# Optimizing a Trainium2 kernel written in Bass

```python
import numpy as np
import jax
import jax.numpy as jnp

def _softmax(x, axis=-1):
    return jax.nn.softmax(x, axis=axis)

def _gelu(x):
    return jax.nn.gelu(x, approximate=True)

def _silu(x):
    return jax.nn.silu(x)

def _sigmoid(x):
    return jax.nn.sigmoid(x)

def _layernorm(x, axis=-1, eps=1e-05):
    m = jnp.mean(x, axis=axis, keepdims=True)
    v = jnp.var(x, axis=axis, keepdims=True)
    return (x - m) / jnp.sqrt(v + eps)

def _scatter_add(tgt, idx, src, axis=0):
    return tgt.at[idx].add(src)

def _segment_sum(src, seg, n):
    return jax.ops.segment_sum(src, seg, n)
kernel_name = 'mk_adj_preln_d1_adj_r2_953be4'

def setup_inputs(seed: int=0):
    np.random.seed(seed)
    _w = jnp.asarray

    def _rec_inputs():
        import jax
        import jax.numpy as jnp
        _gk = jax.random.key(seed)
        x = -0.0005207 + 1.001 * jax.random.normal(jax.random.fold_in(_gk, 1), (8192, 128), jnp.float32)
        _a = jax.random.bernoulli(jax.random.fold_in(_gk, 2), 0.00195312, (8192, 8192))
        adj = _a.astype(jnp.int32)
        return (x, adj)
    x, adj = _rec_inputs()

    def _L0_gnn_setup():
        import jax, jax.numpy as jnp
        import numpy as np
        ALPHA = 0.2
        key = jax.random.key(seed)
        k1, k2, k3, k4 = jax.random.split(key, 4)
        N, Fin, Fout = (4096, 128, 128)
        h = jax.random.normal(k1, (N, Fin), dtype=jnp.float32)
        adj = jax.random.randint(k2, (N, N), 0, 2, dtype=jnp.int32)
        wlim = np.sqrt(6.0 / (Fin + Fout)).astype(np.float32)
        W = jax.random.uniform(k3, (Fin, Fout), dtype=jnp.float32, minval=-wlim, maxval=wlim)
        alim = np.sqrt(6.0 / (2 * Fout + 1)).astype(np.float32)
        a = jax.random.uniform(k4, (2 * Fout, 1), dtype=jnp.float32, minval=-alim, maxval=alim)
        return {'h': h, 'adj': adj, 'W': W, 'a': a}
    _L0_gnn_all = _L0_gnn_setup()
    _L0_gnn_in = {k: v for k, v in _L0_gnn_all.items() if k in ('W', 'a')}
    del _L0_gnn_all
    return {'x': x, 'adj': adj, 'L0_gnn_W': _L0_gnn_in['W'], 'L0_gnn_a': _L0_gnn_in['a']}

def reference(x, adj, L0_gnn_W, L0_gnn_a):
    import jax
    import jax.numpy as jnp

    def _L0_gnn_ref(h, adj, W, a):
        import jax, jax.numpy as jnp
        import numpy as np
        ALPHA = 0.2
        Fout = W.shape[1]
        Wh = h @ W
        a1, a2 = (a[:Fout, 0], a[Fout:, 0])
        f1 = Wh @ a1
        f2 = Wh @ a2
        e = jax.nn.leaky_relu(f1[:, None] + f2[None, :], negative_slope=ALPHA)
        e = jnp.where(adj == 0, -jnp.inf, e)
        attention = jax.nn.softmax(e, axis=1)
        h_prime = attention @ Wh
        return h_prime
    h = jnp.maximum(_layernorm(x, axis=-1), 0.0)
    x = x + _L0_gnn_ref(h, adj, L0_gnn_W, L0_gnn_a)
    return x

_drawn_inputs = setup_inputs


def setup_inputs(seed=0):
    import zlib

    import numpy as np

    out = dict(_drawn_inputs(seed))
    spreads = {}
    factors = {}
    for name, (base, spread) in spreads.items():
        noise = np.random.default_rng([zlib.crc32(name.encode()), seed]).standard_normal(out[name].shape)
        drawn = base * np.exp(spread * noise) if base else spread * noise
        out[name] = jnp.asarray(drawn.astype(out[name].dtype))
    for name, factor in factors.items():
        out[name] = (out[name] * factor).astype(out[name].dtype)
    return out
```

```python
from contextlib import ExitStack

import concourse.bass as bass
from concourse import mybir

ALU = mybir.AluOpType
ACT = mybir.ActivationFunctionType
AX_X = mybir.AxisListType.X
F32 = mybir.dt.float32
F16 = mybir.dt.float16
BF16 = mybir.dt.bfloat16
F8 = mybir.dt.float8e5
I32 = mybir.dt.int32

P = 128
PACK = 4
BANK = 512
CHUNK = PACK * BANK
SLOPE = 0.2
EPS = 1e-5
LOW = 2048.0
TOP = 16384.0
NEG = 3.0e38
SCORE_SCALE = 256.0
ROUND = 12288.0
HALF = 2.0 ** -11
CLAMP = 4000.0
F2_LIMIT = 15.0
SPREAD_LIMIT = 14.0
WH_LIMITS = (2.0 ** -8, 2.0 ** 6)


def gat_kernel(nc, x, adj, W, a, out):
    N, D = x.shape
    Fo = W.shape[1]
    NB = N // P
    NQ = NB // PACK
    NC = N // CHUNK
    QC = CHUNK // (P * PACK)
    GC = PACK * NC
    E1 = Fo + 1
    WC = Fo + 2
    assert D == P and Fo == P and N % CHUNK == 0 and 2 * WC * 2 == WC * 4

    with ExitStack() as ctx:
        def sb(name, shape, dt):
            return ctx.enter_context(nc.sbuf_tensor(name, shape, dt))

        def ps(name, shape, dt):
            return ctx.enter_context(nc.psum_tensor(name, shape, dt))

        def sem(name):
            return ctx.enter_context(nc.semaphore(name))

        x_sb = sb("x_sb", [P, NB, D], F32)
        wh = sb("wh", [P, NB, WC], F32)
        pos = wh.bitcast(F16)
        ht = sb("ht", [P, NB, WC], F32)
        neg = ht.bitcast(F16)
        f2row = sb("f2row", [P, N], F32)
        adj_sb = sb("adj_sb", [P, NC, CHUNK], I32)
        code = sb("code", [P, 2, CHUNK], F8)
        codet = sb("codet", [P, 2, CHUNK], BF16)
        mpos = sb("mpos", [P, 2, CHUNK], F16)
        mneg = sb("mneg", [P, 2, CHUNK], F16)
        ident = sb("ident", [P, P], F32)
        wx = sb("wx", [P, WC], F32)
        wt = sb("wt", [P, P], F32)
        a_sb = sb("a_sb", [P, 2], F32)
        wa2 = sb("wa2", [P, P], F32)
        stats = sb("stats", [P, NB, 6], F32)
        mean = sb("mean", [P, NB], F32)
        rstd = sb("rstd", [P, NB], F32)
        small = sb("small", [P, 4, NB], F32)
        low = sb("low", [P, 2], F32)
        lim = sb("lim", [P, 4], F32)
        glim = sb("glim", [P, 4], F32)
        gs = sb("gs", [P, 8], F32)
        flag = sb("flag", [P, 1], I32)
        f1q = sb("f1q", [P, NB], F32)
        f1c = sb("f1c", [P, 2], F32)
        us = sb("us", [P, NB], F32)
        vs = sb("vs", [P, NB], F32)
        U = sb("U", [P, NB], F32)
        V = sb("V", [P, NB], F32)
        Ul = sb("Ul", [P, NB], F32)
        Vl = sb("Vl", [P, NB], F32)
        num = sb("num", [P, 2, E1], F32)
        inv = sb("inv", [P, 2], F32)
        tmp = sb("tmp", [P, 2, PACK, E1], F32)
        gm = sb("gm", [P, 6], F32)
        drop = mpos.bitcast(F32)
        score = mneg.bitcast(F32)
        probt = codet.bitcast(F32)

        acc = ps("acc", [P, 4, BANK], F32)
        stage = ps("stage", [P, 4, BANK], F32)

        s = {n: sem(n) for n in (
            "x_loaded0", "x_loaded1", "x_loaded2", "x_loaded3", "w_loaded", "a_loaded",
            "adj_loaded0", "adj_loaded1", "adj_loaded2", "adj_loaded3",
            "ident_zero", "ident_ready", "chunk_read", "rows_done", "out_stored",
            "dve_step", "act_step", "limits_ready", "limits_reduced", "flag_ready",
            "sqrt_ready", "var_ready", "xn_ready", "xt_ready", "ht_ready", "whp_ready", "wh_ready",
            "rowp_ready", "row_ready", "wtp_ready", "wt_ready", "wap_ready", "wx_ready",
            "exps_ready", "exparg_ready", "scaled_ready", "high_ready", "pos_ready", "neg_ready",
            "f1_ready", "transposed", "evacuated", "masks_ready", "masks_used", "sums_ready", "first_term",
            "term_ready", "g_step", "g_row", "g_rowp", "g_shift", "g_probs", "g_tp", "g_t", "g_sums")}
        adj_loaded = [s[f"adj_loaded{c}"] for c in range(NC)]
        x_loaded = [s[f"x_loaded{c}"] for c in range(4)]

        x_dram = x.rearrange("(q p s) d -> p q (s d)", p=P, s=PACK)
        out_dram = out.rearrange("(q p s) d -> p q (s d)", p=P, s=PACK)
        adj_dram = adj.rearrange("(q p s) (c k) -> q s c p k", p=P, s=PACK, k=CHUNK)
        xq = x_sb[:].rearrange("p (q s) d -> p q (s d)", s=PACK)
        XP = NQ // 4

        htb = ht[:].rearrange("p t c -> p (t c)")[:, 0:N].rearrange("p (t k) -> p t k", k=P)
        xn = wh[:].rearrange("p t c -> p (t c)")[:, 0:N].rearrange("p (t k) -> p t k", k=P)
        f2q = f2row[:].rearrange("p (q k s) -> p q s k", k=P, s=PACK)
        dropv = drop[:].rearrange("p a b -> p (a b)")
        scorev = score[:].rearrange("p a b -> p (a b)")
        probtv = probt[:].rearrange("p a (b c) -> p (a b) c", c=BANK)
        expo = htb.rearrange("p t k -> p (t k)")
        expoq = expo.rearrange("p (q k s) -> p q s k", k=P, s=PACK)
        posv = pos[:].rearrange("p t (h c) -> p t h c", h=2)
        negv = neg[:].rearrange("p t (h c) -> p t h c", h=2)

        block = ctx.enter_context(nc.Block())

        @block.sync
        def _(sp):
            for k in range(4):
                sp.dma_start(xq[:, k * XP:(k + 1) * XP, :],
                             x_dram[:, k * XP:(k + 1) * XP, :]).then_inc(x_loaded[k], 16)
            sp.dma_start(wx[:, 0:Fo], W).then_inc(s["w_loaded"], 16)
            with nc.allow_non_contiguous_dma(reason="the 256 values of a, once"):
                sp.dma_start(a_sb[:], a.rearrange("(c f) o -> f (c o)", c=2)).then_inc(s["a_loaded"], 16)

            def load(q, r, c):
                sp.dma_start(adj_sb[:, c, :], adj_dram[q, r, c]).then_inc(adj_loaded[c], 16)

            for c in range(NC):
                load(0, 0, c)
            for r in range(1, PACK):
                for c in range(NC):
                    sp.wait_ge(s["chunk_read"], (r - 1) * NC + c + 1)
                    load(0, r, c)
            with sp.Fori(1, NQ) as q:
                for r in range(PACK):
                    for c in range(NC):
                        sp.wait_ge(s["chunk_read"], q * GC + (r - 1) * NC + c + 1)
                        load(q, r, c)
                    if r == 1:
                        sp.wait_ge(s["rows_done"], q * PACK)
                        sp.dma_start(out_dram[:, q - 1, :], xq[:, q - 1, :]).then_inc(s["out_stored"], 16)
            sp.wait_ge(s["rows_done"], NB)
            sp.dma_start(out_dram[:, NQ - 1, :], xq[:, NQ - 1, :]).then_inc(s["out_stored"], 16)
            sp.wait_ge(s["out_stored"], 16 * NQ)

        @block.gpsimd
        def _(pool):
            nc.gpsimd.memset(ident[:], 0.0).then_inc(s["ident_zero"], 1)
            pool.wait_ge(s["ident_zero"], 1)
            nc.gpsimd.affine_select(out=ident[:], in_=ident[:], compare_op=ALU.not_equal, fill=1.0, base=0,
                                    pattern=[[-1, P]], channel_multiplier=1).then_inc(s["ident_ready"], 1)
            pool.wait_ge(s["limits_ready"], 1)
            nc.gpsimd.partition_all_reduce(glim[:], lim[:], P,
                                           bass.bass_isa.ReduceOp.max).then_inc(s["limits_reduced"], 1)

        @block.tensor
        def _(pe):
            pe.wait_ge(s["ident_ready"], 1)
            pe.wait_ge(s["w_loaded"], 16)
            nc.tensor.transpose(acc[:, 0, 0:P], wx[:, 0:Fo], ident[:]).then_inc(s["wtp_ready"], 1)
            pe.wait_ge(s["wt_ready"], 1)
            pe.wait_ge(s["a_loaded"], 16)
            nc.tensor.matmul(acc[:, 1, 0:2], wt[:], a_sb[:], start=True, stop=True).then_inc(s["wap_ready"], 1)
            for q in range(NQ):
                pe.wait_ge(s["xn_ready"], q + 1)
                if q >= 4:
                    pe.wait_ge(s["ht_ready"], q - 3)
                for r in range(PACK):
                    mm = nc.tensor.transpose(stage[:, q % 4, r * P:(r + 1) * P], xn[:, q * PACK + r, :], ident[:])
                mm.then_inc(s["xt_ready"], 1)
            pe.wait_ge(s["wx_ready"], 1)
            pe.wait_ge(s["ht_ready"], NQ)
            for q in range(NQ):
                if q >= 2:
                    pe.wait_ge(s["row_ready"], q - 1)
                nc.tensor.matmul(stage[:, q % 2, :], wa2[:], htb[:, q * PACK:(q + 1) * PACK, :],
                                 start=True, stop=True).then_inc(s["rowp_ready"], 1)
            for q in range(NQ):
                if q >= 2:
                    pe.wait_ge(s["wh_ready"], q - 1)
                for r in range(PACK):
                    o = acc[:, 2 * (q % 2) + r // 2, (r % 2) * 256:(r % 2) * 256 + WC]
                    mm = nc.tensor.matmul(o, htb[:, q * PACK + r, :], wx[:], start=(r % 2 == 0), stop=(r % 2 == 1),
                                          skip_group_check=True)
                mm.then_inc(s["whp_ready"], 1)

            pe.wait_ge(s["flag_ready"], 1)
            fast = pe.value_load(flag[0:1, 0:1], min_val=0, max_val=1)

            def transposes(n, b):
                pe.wait_ge(s["chunk_read"], n + 1)
                pe.wait_ge(s["evacuated"], n - 3)
                for k in range(QC):
                    mm = nc.tensor.transpose(stage[:, b % 4, k * P:(k + 1) * P],
                                             code[:, b % 2, :].bitcast(F32)[:, k * P:(k + 1) * P], ident[:])
                mm.then_inc(s["transposed"], 1)

            def products(n, b, rb, first=False):
                pe.wait_ge(s["masks_ready"], n + 1)
                c, parity = b % NC, (b // NC) % 2
                if c == 0 and not first:
                    pe.wait_ge(s["rows_done"], rb - 1)
                for k in range(QC):
                    for r in range(PACK):
                        t = (c * QC + k) * PACK + r
                        w = slice((r * QC + k) * P, (r * QC + k + 1) * P)
                        st, sp_ = (c == 0 and k == 0 and r == 0), (c == NC - 1 and k == QC - 1 and r == PACK - 1)
                        nc.tensor.matmul(acc[:, 2 * parity, 0:2 * E1], mpos[:, b % 2, w], posv[:, t, :, 0:E1],
                                         start=st, stop=sp_)
                        mm = nc.tensor.matmul(acc[:, 2 * parity + 1, 0:2 * E1], mneg[:, b % 2, w],
                                              negv[:, t, :, 0:E1], start=st, stop=sp_)
                mm.then_inc(s["masks_used"], 1)

            with pe.If(fast):
                for b in range(2):
                    pe.wait_ge(s["chunk_read"], b + 1)
                    if b == 0:
                        pe.wait_ge(s["row_ready"], NQ)
                    for k in range(QC):
                        mm = nc.tensor.transpose(stage[:, b % 4, k * P:(k + 1) * P],
                                                 code[:, b % 2, :].bitcast(F32)[:, k * P:(k + 1) * P], ident[:])
                    mm.then_inc(s["transposed"], 1)
                pe.wait_ge(s["wh_ready"], NQ)
                pe.wait_ge(s["neg_ready"], NQ)

                def chunk(n, b, rb, first, ahead=True):
                    if ahead:
                        if first and b < 2:
                            pe.wait_ge(s["chunk_read"], b + 3)
                            for k in range(QC):
                                mm = nc.tensor.transpose(stage[:, (b + 2) % 4, k * P:(k + 1) * P],
                                                         code[:, b % 2, :].bitcast(F32)[:, k * P:(k + 1) * P],
                                                         ident[:])
                            mm.then_inc(s["transposed"], 1)
                        else:
                            transposes(n + 2, b + 2)
                    products(n, b, rb, first and b < 2 * NC)

                for b in range(GC):
                    chunk(b, b, b // NC, True)
                with pe.Fori(1, NQ - 1) as q:
                    for b in range(GC):
                        chunk(q * GC + b, b, q * PACK + b // NC, False)
                for b in range(GC):
                    chunk((NQ - 1) * GC + b, b, (NQ - 1) * PACK + b // NC, False, ahead=b < GC - 2)
            with pe.Else():
                for q in range(NQ):
                    if q == 0:
                        pe.wait_ge(s["row_ready"], NQ)
                    if q >= 2:
                        pe.wait_ge(s["g_row"], q - 1)
                    nc.tensor.matmul(stage[:, q % 2, :], wa2[:], htb[:, q * PACK:(q + 1) * PACK, :],
                                     start=True, stop=True).then_inc(s["g_rowp"], 1)
                pe.wait_ge(s["g_row"], NQ)
                with pe.Fori(0, NB) as t:
                    pe.wait_ge(s["g_probs"], t + 1)
                    for q in range(NQ):
                        if q >= 4:
                            pe.wait_ge(s["g_t"], t * NQ + q - 3)
                        for r in range(PACK):
                            mm = nc.tensor.transpose(stage[:, q % 4, r * P:(r + 1) * P], expoq[:, q, r, :], ident[:])
                        mm.then_inc(s["g_tp"], 1)
                        pe.wait_ge(s["g_t"], t * NQ + q + 1)
                        for r in range(PACK):
                            mm = nc.tensor.matmul(acc[:, 0, 0:Fo], probtv[:, q % 4, r * P:(r + 1) * P],
                                                  wh[:, q * PACK + r, 0:Fo], start=(q == 0 and r == 0),
                                                  stop=(q == NQ - 1 and r == PACK - 1))
                    mm.then_inc(s["g_sums"], 1)

        @block.scalar
        def _(act):
            act.wait_ge(s["wtp_ready"], 1)
            nc.scalar.activation(wt[:], acc[:, 0, 0:P], ACT.Copy).then_inc(s["wt_ready"], 1)
            act.wait_ge(s["var_ready"], 1)
            nc.scalar.activation(small[:, 1, :], small[:, 0, :], ACT.Sqrt).then_inc(s["sqrt_ready"], 1)
            for q in range(NQ):
                act.wait_ge(s["xt_ready"], q + 1)
                nc.scalar.activation(htb[:, q * PACK:(q + 1) * PACK, :],
                                     stage[:, q % 4, :].rearrange("p (t k) -> p t k", k=P),
                                     ACT.Relu).then_inc(s["ht_ready"], 1)
            for q in range(NQ):
                act.wait_ge(s["whp_ready"], q + 1)
                o = wh[:, q * PACK:(q + 1) * PACK, :].rearrange("p (b r) c -> p b r c", b=2)
                i = acc[:, 2 * (q % 2):2 * (q % 2) + 2, :].rearrange("p b (r c) -> p b r c", r=2)[:, :, :, 0:WC]
                for b in range(2):
                    mm = nc.scalar.activation(o[:, b], i[:, b], ACT.Copy)
                mm.then_inc(s["wh_ready"], 1)
            act.wait_ge(s["flag_ready"], 1)
            fast = act.value_load(flag[0:1, 0:1], min_val=0, max_val=1)
            with act.If(fast):
                act.wait_ge(s["exparg_ready"], 1)
                for k, o in enumerate((us, vs, U, V)):
                    ins = nc.scalar.activation(o[:], small[:, k, :], ACT.Exp)
                ins.then_inc(s["exps_ready"], 1)
                for k in range(2 * NQ):
                    q, parts = k // 2, (posv, negv)[1 - k % 2]
                    act.wait_ge(s["scaled_ready"], k + 1)
                    nc.scalar.activation(parts[:, q * PACK:(q + 1) * PACK, 0, 0:E1], tmp[:, k % 2],
                                         ACT.Copy, scale=1.0 / LOW).then_inc(s["high_ready"], 1)

                turned = act.alloc_register("transposed_count")
                masked = act.alloc_register("masks_ready_count")

                def evacuate(b, n=None):
                    if n is None:
                        act.wait_ge(s["transposed"], turned)
                        act.wait_ge(s["masks_ready"], masked)
                        act.reg_add(turned, turned, 1)
                        act.reg_add(masked, masked, 1)
                    else:
                        act.wait_ge(s["transposed"], n + 1)
                        if n >= 2:
                            act.wait_ge(s["masks_ready"], n - 1)
                    nc.scalar.activation(
                        codet[:, b % 2, :].rearrange("p (s w) -> p s w", s=PACK),
                        stage[:, b % 4, :].bitcast(F8).rearrange("p (w s) -> p s w", s=PACK),
                        ACT.Copy).then_inc(s["evacuated"], 1)

                def first_term(rb, parity, t):
                    act.wait_ge(s["masks_used"], (rb + 1) * NC)
                    nc.scalar.activation(num[:, parity, :], acc[:, 2 * parity, 0:E1], ACT.Copy,
                                         scale=U[:, bass.ds(t, 1)]).then_inc(s["first_term"], 1)

                for b in range(GC):
                    evacuate(b, b)
                    if b % NC == 1 and b > NC:
                        first_term(b // NC - 1, (b // NC - 1) % 2, b // NC - 1)
                act.reg_mov(turned, GC + 1)
                act.reg_mov(masked, GC - 1)
                with act.Fori(1, NQ) as q:
                    for b in range(GC):
                        evacuate(b)
                        if b % NC == 1:
                            first_term(q * PACK + b // NC - 1, (b // NC - 1) % 2, q * PACK + b // NC - 1)
                first_term(NB - 1, (NB - 1) % 2, NB - 1)
            with act.Else():
                for q in range(NQ):
                    act.wait_ge(s["g_rowp"], q + 1)
                    nc.scalar.activation(f2q[:, q], stage[:, q % 2, :].rearrange("p (s k) -> p s k", k=P), ACT.Copy,
                                         scale=1.0 / SCORE_SCALE).then_inc(s["g_row"], 1)
                with act.Fori(0, NB) as t:
                    act.wait_ge(s["g_shift"], t + 1)
                    nc.scalar.activation(expo, expo, ACT.Exp, bias=gm[:, 1:2],
                                         accum_out=gm[:, 2:3]).then_inc(s["g_probs"], 1)
                    for q in range(NQ):
                        act.wait_ge(s["g_tp"], t * NQ + q + 1)
                        nc.scalar.activation(probtv[:, q % 4, :], stage[:, q % 4, :], ACT.Copy).then_inc(s["g_t"], 1)

        @block.vector
        def _(dve):
            steps = [0]

            def then(ins):
                steps[0] += 1
                ins.then_inc(s["dve_step"], 1)
                dve.wait_ge(s["dve_step"], steps[0])

            for t in range(NB):
                if t % (NB // 4) == 0:
                    dve.wait_ge(x_loaded[t // (NB // 4)], 16)
                ins = nc.vector.bn_stats(stats[:, t, :], x_sb[:, t, :])
            then(ins)
            me, mo = stats[:, :, 1], stats[:, :, 4]
            then(nc.vector.tensor_tensor(small[:, 0, :], me, mo, ALU.subtract))
            then(nc.vector.tensor_tensor(mean[:], me, mo, ALU.add))
            then(nc.vector.tensor_scalar(mean[:], mean[:], 0.5, None, ALU.mult))
            then(nc.vector.tensor_tensor(small[:, 1, :], small[:, 0, :], small[:, 0, :], ALU.mult))
            then(nc.vector.tensor_tensor(small[:, 2, :], stats[:, :, 2], stats[:, :, 5], ALU.add))
            then(nc.vector.tensor_scalar(small[:, 3, :], small[:, 1, :], 0.25, EPS, ALU.mult, ALU.add))
            nc.vector.scalar_tensor_tensor(out=small[:, 0, :], in0=small[:, 2, :], scalar=1.0 / D,
                                           in1=small[:, 3, :], op0=ALU.mult, op1=ALU.add
                                           ).then_inc(s["var_ready"], 1)
            dve.wait_ge(s["sqrt_ready"], 1)
            then(nc.vector.reciprocal(rstd[:], small[:, 1, :]))
            then(nc.vector.tensor_tensor(small[:, 2, :], rstd[:], rstd[:], ALU.mult))
            then(nc.vector.tensor_tensor(small[:, 3, :], small[:, 2, :], small[:, 0, :], ALU.mult))
            then(nc.vector.tensor_scalar(small[:, 2, :], small[:, 3, :], -0.5, 1.5, ALU.mult, ALU.add))
            then(nc.vector.tensor_tensor(rstd[:], rstd[:], small[:, 2, :], ALU.mult))
            for t in range(NB):
                ins = nc.vector.tensor_scalar(xn[:, t, :], x_sb[:, t, :], mean[:, t:t + 1], rstd[:, t:t + 1],
                                              ALU.subtract, ALU.mult)
                if t % PACK == PACK - 1:
                    ins.then_inc(s["xn_ready"], 1)
                if t == PACK - 1:
                    dve.wait_ge(s["wap_ready"], 1)
                    then(nc.vector.tensor_copy(wx[:, Fo:WC], acc[:, 1, 0:2]))
                    nc.vector.tensor_scalar(wa2[:], wx[:, Fo + 1:WC].to_broadcast([P, P]), SCORE_SCALE, None,
                                            ALU.mult).then_inc(s["wx_ready"], 1)
            for q in range(NQ):
                dve.wait_ge(s["rowp_ready"], q + 1)
                nc.vector.tensor_scalar(f2q[:, q], stage[:, q % 2, :].rearrange("p (s k) -> p s k", k=P),
                                        ROUND, ROUND, ALU.add, ALU.subtract).then_inc(s["row_ready"], 1)
            dve.wait_ge(s["wh_ready"], NQ)
            f1, f2 = wh[:, :, Fo], wh[:, :, Fo + 1]
            nc.vector.reduce_max(lim[:, 0:1], f2, AX_X)
            nc.vector.tensor_reduce(low[:, 0:1], f2, AX_X, ALU.min)
            nc.vector.tensor_reduce(lim[:, 2:3], wh[:, :, 0:Fo], mybir.AxisListType.XY, ALU.max)
            then(nc.vector.tensor_reduce(low[:, 1:2], wh[:, :, 0:Fo], mybir.AxisListType.XY, ALU.min))
            nc.vector.tensor_scalar(lim[:, 1:4:2], low[:], -1.0, None, ALU.mult).then_inc(s["limits_ready"], 1)
            then(nc.vector.tensor_scalar(f1q[:], f1, SCORE_SCALE, None, ALU.mult))
            then(nc.vector.tensor_scalar(f1q[:], f1q[:], CLAMP, -CLAMP, ALU.min, ALU.max))
            then(nc.vector.tensor_scalar(f1q[:], f1q[:], ROUND, ROUND, ALU.add, ALU.subtract))
            then(nc.vector.tensor_scalar(f1q[:], f1q[:], HALF, None, ALU.add))
            dve.wait_ge(s["limits_reduced"], 1)
            F, nF, mW = glim[:, 0:1], glim[:, 1:2], gs[:, 7:8]
            then(nc.vector.tensor_tensor(mW, glim[:, 2:3], glim[:, 3:4], ALU.max))
            then(nc.vector.tensor_scalar(gs[:, 0:1], F, nF, SPREAD_LIMIT, ALU.add, ALU.is_le))
            then(nc.vector.tensor_scalar(gs[:, 1:2], F, nF, F2_LIMIT, ALU.max, ALU.is_le))
            then(nc.vector.tensor_scalar(gs[:, 2:3], mW, WH_LIMITS[1], gs[:, 1:2], ALU.is_le, ALU.mult))
            then(nc.vector.tensor_scalar(gs[:, 3:4], mW, WH_LIMITS[0], gs[:, 2:3], ALU.is_ge, ALU.mult))
            nc.vector.tensor_scalar(flag[:], gs[:, 3:4], gs[:, 0:1], None, ALU.mult).then_inc(s["flag_ready"], 1)
            dve.wait_ge(s["flag_ready"], 1)
            fast = dve.value_load(flag[0:1, 0:1], min_val=0, max_val=1)
            with dve.If(fast):
                then(nc.vector.tensor_scalar(gs[:, 4:5], mW, 1.0, None, ALU.max))
                then(nc.vector.reciprocal(gs[:, 5:6], gs[:, 4:5]))
                then(nc.vector.tensor_scalar(gs[:, 6:7], gs[:, 5:6], TOP * LOW, None, ALU.mult))
                then(nc.vector.tensor_scalar(small[:, 0, :], f2, F, None, ALU.subtract))
                then(nc.vector.tensor_scalar(small[:, 1, :], small[:, 0, :], SLOPE, None, ALU.mult))
                then(nc.vector.tensor_scalar(Ul[:], f1, F, None, ALU.add))
                then(nc.vector.tensor_scalar(small[:, 2, :], Ul[:], 0.0, 1.0 - SLOPE, ALU.min, ALU.mult))
                nc.vector.tensor_scalar(small[:, 3, :], Ul[:], 0.0, -(1.0 - SLOPE), ALU.max, ALU.mult
                                        ).then_inc(s["exparg_ready"], 1)
                dve.wait_ge(s["exps_ready"], 1)
                then(nc.vector.tensor_scalar(us[:], us[:], gs[:, 6:7], None, ALU.mult))
                then(nc.vector.tensor_scalar(vs[:], vs[:], gs[:, 6:7], None, ALU.mult))
                nc.vector.tensor_scalar(Ul[:], U[:], 1.0 / LOW, None, ALU.mult)
                then(nc.vector.tensor_scalar(Vl[:], V[:], 1.0 / LOW, None, ALU.mult))
                then(nc.vector.memset(wh[:, :, Fo:E1], 1.0))

                def scaled(k):
                    q, c = k // 2, (us, vs)[1 - k % 2]
                    sl = slice(q * PACK, (q + 1) * PACK)
                    nc.vector.tensor_tensor(tmp[:, k % 2], wh[:, sl, 0:E1],
                                            c[:, sl].unsqueeze(2).to_broadcast([P, PACK, E1]),
                                            ALU.mult).then_inc(s["scaled_ready"], 1)

                def low_parts(k):
                    q, parts, done = k // 2, (posv, negv)[1 - k % 2], (s["pos_ready"], s["neg_ready"])[1 - k % 2]
                    dve.wait_ge(s["high_ready"], k + 1)
                    sl = slice(q * PACK, (q + 1) * PACK)
                    nc.vector.scalar_tensor_tensor(out=parts[:, sl, 1, 0:E1], in0=parts[:, sl, 0, 0:E1],
                                                   scalar=-LOW, in1=tmp[:, k % 2], op0=ALU.mult,
                                                   op1=ALU.add).then_inc(done, 1)

                for q in range(NQ):
                    if q >= 1:
                        dve.wait_ge(s["pos_ready"], q)
                    scaled(2 * q)
                    scaled(2 * q + 1)
                    dve.wait_ge(s["scaled_ready"], 2 * q + 2)
                    low_parts(2 * q)
                    low_parts(2 * q + 1)

                def f1_column(t, rb):
                    nc.vector.tensor_copy(f1c[:, rb % 2:rb % 2 + 1], f1q[:, bass.ds(t, 1)]
                                          ).then_inc(s["f1_ready"], 1)

                turned = dve.alloc_register("transposed_count")

                def codes(n, b, t, first=False, last=False, final=False):
                    c, rb = b % NC, b // NC
                    dve.wait_ge(adj_loaded[c], 16 * (t + 1))
                    if c == 0:
                        dve.wait_ge(s["f1_ready"], t + 1)
                    if first or last:
                        if not (first and b < 2):
                            dve.wait_ge(s["transposed"], n - 1)
                    else:
                        dve.wait_ge(s["transposed"], turned)
                        dve.reg_add(turned, turned, 1)
                    nc.vector.scalar_tensor_tensor(out=code[:, b % 2, :], in0=f2row[:, c * CHUNK:(c + 1) * CHUNK],
                                                   scalar=f1c[:, rb % 2:rb % 2 + 1], in1=adj_sb[:, c, :],
                                                   op0=ALU.add, op1=ALU.mult, saturate=False
                                                   ).then_inc(s["chunk_read"], 1)
                    if c == NC - 2 and not final:
                        f1_column(t + 1, rb + 1)

                def masks(n, b, first=False):
                    dve.wait_ge(s["evacuated"], n + 1)
                    if not first:
                        dve.wait_ge(s["masks_used"], n - 1)
                    nc.vector.tensor_scalar(mpos[:, b % 2, :], codet[:, b % 2, :], 0.0, None, ALU.is_gt)
                    nc.vector.tensor_scalar(mneg[:, b % 2, :], codet[:, b % 2, :], 0.0, None, ALU.is_lt
                                            ).then_inc(s["masks_ready"], 1)

                def finish(step, rb, parity):
                    r, t = num[:, parity, :], rb
                    if step == 0:
                        dve.wait_ge(s["first_term"], rb + 1)
                        ins = nc.vector.scalar_tensor_tensor(out=r, in0=acc[:, 2 * parity, E1:2 * E1],
                                                             scalar=Ul[:, bass.ds(t, 1)], in1=r,
                                                             op0=ALU.mult, op1=ALU.add)
                    else:
                        dve.wait_ge(s["term_ready"], 4 * rb + step)
                    if step in (1, 2):
                        f, o = ((V, 0), (Vl, E1))[step - 1]
                        ins = nc.vector.scalar_tensor_tensor(out=r, in0=acc[:, 2 * parity + 1, o:o + E1],
                                                             scalar=f[:, bass.ds(t, 1)], in1=r,
                                                             op0=ALU.mult, op1=ALU.add)
                    if step == 3:
                        ins = nc.vector.reciprocal(inv[:, parity:parity + 1], num[:, parity, Fo:E1])
                    if step < 4:
                        ins.then_inc(s["term_ready"], 1)
                    else:
                        xt = x_sb[:, bass.ds(t, 1), :].rearrange("p o d -> p (o d)")
                        nc.vector.scalar_tensor_tensor(out=xt, in0=num[:, parity, 0:Fo],
                                                       scalar=inv[:, parity:parity + 1], in1=xt,
                                                       op0=ALU.mult, op1=ALU.add).then_inc(s["rows_done"], 1)

                def chunk(n, b, base, first=False, ahead=True, last=False):
                    rb = b // NC
                    if ahead:
                        codes(n + 3, b + 3, base + (b + 3) // NC, first, last, last and b + 3 >= GC - NC)
                    done = not (first and rb == 0)
                    if done and b % NC >= 2:
                        finish(2 * (b % NC) - 3, base + rb - 1, (rb - 1) % 2)
                    masks(n, b, first=first and b < 2)
                    if done and b % NC >= 1:
                        finish(2 * (b % NC) - 2, base + rb - 1, (rb - 1) % 2)

                f1_column(0, 0)
                for b in range(3):
                    codes(b, b, 0, first=True)
                for b in range(GC):
                    chunk(b, b, 0, first=True)
                dve.reg_mov(turned, GC + 2)
                with dve.Fori(1, NQ - 1) as q:
                    for b in range(GC):
                        chunk(q * GC + b, b, q * PACK)
                for b in range(GC):
                    chunk((NQ - 1) * GC + b, b, (NQ - 1) * PACK, ahead=b < GC - 3, last=True)
                for st in range(5):
                    finish(st, NB - 1, (NB - 1) % 2)
            with dve.Else():
                dve.wait_ge(s["g_row"], NQ)
                GS = 3 * NC + 5
                with dve.Fori(0, NB) as t:
                    f1t = wh[:, bass.ds(t, 1), Fo:E1].rearrange("p o c -> p (o c)")
                    for c in range(NC):
                        sl = slice(c * CHUNK, (c + 1) * CHUNK)
                        dve.wait_ge(adj_loaded[c], 16 * (t + 1))
                        nc.vector.tensor_scalar(dropv, adj_sb[:, c, :], 1.0, NEG, ALU.subtract, ALU.mult
                                                ).then_inc(s["chunk_read"], 1)
                        nc.vector.tensor_scalar(scorev, f2row[:, sl], f1t, None, ALU.add).then_inc(s["g_step"], 1)
                        dve.wait_ge(s["g_step"], t * GS + 3 * c + 1)
                        nc.vector.scalar_tensor_tensor(out=scorev, in0=scorev, scalar=SLOPE, in1=scorev,
                                                       op0=ALU.mult, op1=ALU.max).then_inc(s["g_step"], 1)
                        dve.wait_ge(s["g_step"], t * GS + 3 * c + 2)
                        dve.wait_ge(s["chunk_read"], t * NC + c + 1)
                        nc.vector.tensor_tensor(expo[:, sl], scorev, dropv, ALU.add).then_inc(s["g_step"], 1)
                        dve.wait_ge(s["g_step"], t * GS + 3 * c + 3)
                    nc.vector.reduce_max(gm[:, 0:1], expo, AX_X).then_inc(s["g_step"], 1)
                    dve.wait_ge(s["g_step"], t * GS + 3 * NC + 1)
                    nc.vector.tensor_scalar(gm[:, 1:2], gm[:, 0:1], -1.0, None, ALU.mult).then_inc(s["g_shift"], 1)
                    nc.vector.tensor_scalar(gm[:, 3:4], gm[:, 0:1], -NEG / 2, None, ALU.is_gt
                                            ).then_inc(s["g_step"], 1)
                    dve.wait_ge(s["g_step"], t * GS + 3 * NC + 2)
                    dve.wait_ge(s["g_sums"], t + 1)
                    nc.vector.tensor_tensor(gm[:, 4:5], gm[:, 2:3], gm[:, 3:4], ALU.mult).then_inc(s["g_step"], 1)
                    dve.wait_ge(s["g_step"], t * GS + 3 * NC + 3)
                    nc.vector.reciprocal(gm[:, 5:6], gm[:, 4:5]).then_inc(s["g_step"], 1)
                    nc.vector.tensor_scalar(num[:, 0, 0:Fo], acc[:, 0, 0:Fo], gm[:, 3:4], None, ALU.mult
                                            ).then_inc(s["g_step"], 1)
                    dve.wait_ge(s["g_step"], t * GS + 3 * NC + 5)
                    xt = x_sb[:, bass.ds(t, 1), :].rearrange("p o d -> p (o d)")
                    nc.vector.scalar_tensor_tensor(out=xt, in0=num[:, 0, 0:Fo], scalar=gm[:, 5:6], in1=xt,
                                                   op0=ALU.mult, op1=ALU.add).then_inc(s["rows_done"], 1)


_INS = ["x", "adj", "L0_gnn_W", "L0_gnn_a"]


def kernel(**inputs):
    import numpy as _np
    import concourse.bacc as _bacc
    from concourse import mybir as _mybir
    from concourse.bass_utils import run_bass_kernel_spmd as _run

    nc = _bacc.Bacc("TRN2", target_bir_lowering=False, num_devices=1)
    arrays, args = {}, []
    for name in _INS:
        v = _np.ascontiguousarray(inputs[name])
        arrays[f"in_{name}_dram"] = v
        args.append(nc.dram_tensor(f"in_{name}_dram", v.shape, _mybir.dt.from_np(v.dtype), kind="ExternalInput").ap())
    shape = inputs["x"].shape
    args.append(nc.dram_tensor("out_0_dram", shape, _mybir.dt.float32, kind="ExternalOutput").ap())
    gat_kernel(nc, *args)
    r = _run(nc, [arrays], core_ids=[0])
    return r.results[0]["out_0_dram"]
```

```python
from contextlib import ExitStack

import concourse.bass as bass
from concourse import mybir

ALU = mybir.AluOpType
ACT = mybir.ActivationFunctionType
AX_X = mybir.AxisListType.X
F32 = mybir.dt.float32
F16 = mybir.dt.float16
BF16 = mybir.dt.bfloat16
F8 = mybir.dt.float8e5
I32 = mybir.dt.int32

P = 128
PACK = 4
BANK = 512
CHUNK = PACK * BANK
SLOPE = 0.2
EPS = 1e-5
LOW = 2048.0
TOP = 16384.0
NEG = 3.0e38
SCORE_SCALE = 256.0
ROUND = 12288.0
HALF = 2.0 ** -11
CLAMP = 4000.0
F2_LIMIT = 15.0
SPREAD_LIMIT = 14.0
WH_LIMITS = (2.0 ** -8, 2.0 ** 6)


def gat_kernel(nc, x, adj, W, a, out):
    N, D = x.shape
    Fo = W.shape[1]
    NB = N // P
    NQ = NB // PACK
    NC = N // CHUNK
    QC = CHUNK // (P * PACK)
    GC = PACK * NC
    E1 = Fo + 1
    WC = Fo + 2
    assert D == P and Fo == P and N % CHUNK == 0 and 2 * WC * 2 == WC * 4

    with ExitStack() as ctx:
        def sb(name, shape, dt):
            return ctx.enter_context(nc.sbuf_tensor(name, shape, dt))

        def ps(name, shape, dt):
            return ctx.enter_context(nc.psum_tensor(name, shape, dt))

        def sem(name):
            return ctx.enter_context(nc.semaphore(name))

        x_sb = sb("x_sb", [P, NB, D], F32)
        wh = sb("wh", [P, NB, WC], F32)
        pos = wh.bitcast(F16)
        ht = sb("ht", [P, NB, WC], F32)
        neg = ht.bitcast(F16)
        f2row = sb("f2row", [P, N], F32)
        adj_sb = sb("adj_sb", [P, NC, CHUNK], I32)
        code = sb("code", [P, 4, CHUNK], F8)
        codet = sb("codet", [P, 2, CHUNK], BF16)
        mpos = sb("mpos", [P, 2, CHUNK], F16)
        mneg = sb("mneg", [P, 2, CHUNK], F16)
        ident = sb("ident", [P, P], F32)
        wx = sb("wx", [P, WC], F32)
        wt = sb("wt", [P, P], F32)
        a_sb = sb("a_sb", [P, 2], F32)
        wa2 = sb("wa2", [P, P], F32)
        stats = sb("stats", [P, NB, 6], F32)
        mean = sb("mean", [P, NB], F32)
        rstd = sb("rstd", [P, NB], F32)
        small = sb("small", [P, 4, NB], F32)
        low = sb("low", [P, 1], F32)
        norms = sb("norms", [P, 1], F32)
        lim = sb("lim", [P, 3], F32)
        glim = sb("glim", [P, 3], F32)
        gs = sb("gs", [P, 8], F32)
        flag = sb("flag", [P, 1], I32)
        f1q = sb("f1q", [P, NB], F32)
        f1c = sb("f1c", [P, 2], F32)
        us = sb("us", [P, NB], F32)
        vs = sb("vs", [P, NB], F32)
        U = sb("U", [P, NB], F32)
        V = sb("V", [P, NB], F32)
        Ul = sb("Ul", [P, NB], F32)
        Vl = sb("Vl", [P, NB], F32)
        num = sb("num", [P, 2, E1], F32)
        inv = sb("inv", [P, 2], F32)
        tmp = sb("tmp", [P, 2, PACK, E1], F32)
        gm = sb("gm", [P, 6], F32)
        drop = mpos.bitcast(F32)
        score = mneg.bitcast(F32)
        probt = codet.bitcast(F32)

        acc = ps("acc", [P, 4, BANK], F32)
        stage = ps("stage", [P, 4, BANK], F32)

        s = {n: sem(n) for n in (
            "x_loaded0", "x_loaded1", "x_loaded2", "x_loaded3", "w_loaded", "a_loaded",
            "adj_loaded0", "adj_loaded1", "adj_loaded2", "adj_loaded3",
            "ident_zero", "ident_ready", "chunk_read", "rows_done", "out_stored",
            "dve_step", "act_step", "limits_ready", "limits_reduced", "flag_ready",
            "sqrt_ready", "var_ready", "xn_ready", "xt_ready", "ht_ready", "whp_ready", "wh_ready",
            "rowp_ready", "row_ready", "wtp_ready", "wt_ready", "wap_ready", "wx_ready",
            "factors_ready", "norms_ready", "bound_ready", "row_even", "act_masks", "exps_ready", "exparg_ready", "scaled_ready", "high_ready", "pos_ready", "neg_ready",
            "f1_ready", "transposed", "evacuated", "masks_ready", "masks_used", "sums_ready", "first_term",
            "term_ready", "g_step", "g_shift", "g_probs", "g_tp", "g_t", "g_sums")}
        adj_loaded = [s[f"adj_loaded{c}"] for c in range(NC)]
        x_loaded = [s[f"x_loaded{c}"] for c in range(4)]

        x_dram = x.rearrange("(q p s) d -> p q (s d)", p=P, s=PACK)
        out_dram = out.rearrange("(q p s) d -> p q (s d)", p=P, s=PACK)
        adj_dram = adj.rearrange("(q p s) (c k) -> q s c p k", p=P, s=PACK, k=CHUNK)
        xq = x_sb[:].rearrange("p (q s) d -> p q (s d)", s=PACK)
        XP = NQ // 4

        htb = ht[:].rearrange("p t c -> p (t c)")[:, 0:N].rearrange("p (t k) -> p t k", k=P)
        xn = wh[:].rearrange("p t c -> p (t c)")[:, 0:N].rearrange("p (t k) -> p t k", k=P)
        f2q = f2row[:].rearrange("p (q k s) -> p q s k", k=P, s=PACK)
        dropv = drop[:].rearrange("p a b -> p (a b)")
        scorev = score[:].rearrange("p a b -> p (a b)")
        probtv = probt[:].rearrange("p a (b c) -> p (a b) c", c=BANK)
        expo = htb.rearrange("p t k -> p (t k)")
        expoq = expo.rearrange("p (q k s) -> p q s k", k=P, s=PACK)
        posv = pos[:].rearrange("p t (h c) -> p t h c", h=2)
        negv = neg[:].rearrange("p t (h c) -> p t h c", h=2)

        block = ctx.enter_context(nc.Block())

        @block.sync
        def _(sp):
            sp.dma_start(wx[:, 0:Fo], W).then_inc(s["w_loaded"], 16)
            with nc.allow_non_contiguous_dma(reason="the 256 values of a, once"):
                sp.dma_start(a_sb[:], a.rearrange("(c f) o -> f (c o)", c=2)).then_inc(s["a_loaded"], 16)
            for k in range(4):
                sp.dma_start(xq[:, k * XP:(k + 1) * XP, :],
                             x_dram[:, k * XP:(k + 1) * XP, :]).then_inc(x_loaded[k], 16)

            def load(q, r, c):
                sp.dma_start(adj_sb[:, c, :], adj_dram[q, r, c]).then_inc(adj_loaded[c], 16)

            for c in range(NC):
                load(0, 0, c)
            for r in range(1, PACK):
                for c in range(NC):
                    sp.wait_ge(s["chunk_read"], (r - 1) * NC + c + 1)
                    load(0, r, c)
            with sp.Fori(1, NQ) as q:
                for r in range(PACK):
                    for c in range(NC):
                        sp.wait_ge(s["chunk_read"], q * GC + (r - 1) * NC + c + 1)
                        load(q, r, c)
                    if r == 1:
                        sp.wait_ge(s["rows_done"], q * PACK)
                        sp.dma_start(out_dram[:, q - 1, :], xq[:, q - 1, :]).then_inc(s["out_stored"], 16)
            sp.wait_ge(s["rows_done"], NB)
            sp.dma_start(out_dram[:, NQ - 1, :], xq[:, NQ - 1, :]).then_inc(s["out_stored"], 16)
            sp.wait_ge(s["out_stored"], 16 * NQ)

        @block.gpsimd
        def _(pool):
            nc.gpsimd.memset(ident[:], 0.0).then_inc(s["ident_zero"], 1)
            pool.wait_ge(s["ident_zero"], 1)
            nc.gpsimd.affine_select(out=ident[:], in_=ident[:], compare_op=ALU.not_equal, fill=1.0, base=0,
                                    pattern=[[-1, P]], channel_multiplier=1).then_inc(s["ident_ready"], 1)
            pool.wait_ge(s["limits_ready"], 1)
            pool.wait_ge(s["bound_ready"], 1)
            nc.gpsimd.partition_all_reduce(glim[:], lim[:], P,
                                           bass.bass_isa.ReduceOp.max).then_inc(s["limits_reduced"], 1)
            pool.wait_ge(s["flag_ready"], 1)
            fast = pool.value_load(flag[0:1, 0:1], min_val=0, max_val=1)
            with pool.If(fast):
                pool.wait_ge(s["factors_ready"], 1)
                for k in range(2 * NQ):
                    sl, c = slice(k // 2 * PACK, (k // 2 + 1) * PACK), (vs, us)[k % 2]
                    if k >= 2:
                        pool.wait_ge((s["neg_ready"], s["pos_ready"])[k % 2], k // 2)
                    nc.gpsimd.tensor_tensor(tmp[:, k % 2], wh[:, sl, 0:E1],
                                            c[:, sl].unsqueeze(2).to_broadcast([P, PACK, E1]),
                                            ALU.mult).then_inc(s["scaled_ready"], 1)
            with pool.Else():
                pass

        @block.tensor
        def _(pe):
            pe.wait_ge(s["ident_ready"], 1)
            pe.wait_ge(s["w_loaded"], 16)
            nc.tensor.transpose(acc[:, 0, 0:P], wx[:, 0:Fo], ident[:]).then_inc(s["wtp_ready"], 1)
            pe.wait_ge(s["wt_ready"], 1)
            pe.wait_ge(s["a_loaded"], 16)
            nc.tensor.matmul(acc[:, 1, 0:2], wt[:], a_sb[:], start=True, stop=True).then_inc(s["wap_ready"], 1)
            for q in range(NQ + 1):
                if q < NQ:
                    pe.wait_ge(s["xn_ready"], q + 1)
                    if q >= 2:
                        pe.wait_ge(s["ht_ready"], q - 1)
                    for r in range(PACK):
                        mm = nc.tensor.transpose(stage[:, q % 2, r * P:(r + 1) * P], xn[:, q * PACK + r, :],
                                                 ident[:])
                    mm.then_inc(s["xt_ready"], 1)
                if q >= 1:
                    g = q - 1
                    if g == 0:
                        pe.wait_ge(s["wx_ready"], 1)
                    pe.wait_ge(s["ht_ready"], g + 1)
                    if g >= 2:
                        pe.wait_ge(s["wh_ready"], g - 1)
                    for r in range(PACK):
                        o = acc[:, 2 * (g % 2) + r // 2, (r % 2) * 256:(r % 2) * 256 + WC]
                        mm = nc.tensor.matmul(o, htb[:, g * PACK + r, :], wx[:], start=(r % 2 == 0),
                                              stop=(r % 2 == 1), skip_group_check=True)
                    mm.then_inc(s["whp_ready"], 1)

            def row(q):
                if q == 0:
                    pe.wait_ge(s["wh_ready"], NQ)
                if q >= 2:
                    pe.wait_ge(s["row_ready"], q - 1)
                nc.tensor.matmul(acc[:, 2 + q % 2, :], wa2[:], htb[:, q * PACK:(q + 1) * PACK, :],
                                 start=True, stop=True).then_inc(s["rowp_ready"], 1)

            for q in range(2):
                row(q)
            pe.wait_ge(s["flag_ready"], 1)
            fast = pe.value_load(flag[0:1, 0:1], min_val=0, max_val=1)

            def transposes(n, b, first=False):
                pe.wait_ge(s["chunk_read"], n + 1)
                if not (first and b < 4):
                    pe.wait_ge(s["evacuated"], n - 3)
                for k in range(QC):
                    mm = nc.tensor.transpose(stage[:, b % 4, k * P:(k + 1) * P],
                                             code[:, b % 4, :].bitcast(F32)[:, k * P:(k + 1) * P], ident[:])
                mm.then_inc(s["transposed"], 1)

            def products(n, b, rb, odd, first=False):
                pe.wait_ge(s["masks_ready"], n + 1)
                if b % 2:
                    pe.wait_ge(s["act_masks"], odd)
                c, parity = b % NC, (b // NC) % 2
                if first and b == NC:
                    pe.wait_ge(s["row_ready"], NQ)
                if c == 0 and not (first and b < 2 * NC):
                    pe.wait_ge(s["rows_done"], rb - 1)
                for k in range(QC):
                    for r in range(PACK):
                        t = (c * QC + k) * PACK + r
                        w = slice((r * QC + k) * P, (r * QC + k + 1) * P)
                        if first and rb == 0 and r == 0:
                            pe.wait_ge(s["neg_ready"], c * QC + k + 1)
                            pe.wait_ge(s["pos_ready"], c * QC + k + 1)
                        st, sp_ = (c == 0 and k == 0 and r == 0), (c == NC - 1 and k == QC - 1 and r == PACK - 1)
                        nc.tensor.matmul(acc[:, 2 * parity, 0:2 * E1], mpos[:, b % 2, w], posv[:, t, :, 0:E1],
                                         start=st, stop=sp_)
                        mm = nc.tensor.matmul(acc[:, 2 * parity + 1, 0:2 * E1], mneg[:, b % 2, w],
                                              negv[:, t, :, 0:E1], start=st, stop=sp_)
                mm.then_inc(s["masks_used"], 1)

            with pe.If(fast):
                for q in range(2, 2 * QC):
                    row(q)
                transposes(0, 0, first=True)
                for q in range(2 * QC, 3 * QC):
                    row(q)
                transposes(1, 1, first=True)
                for q in range(3 * QC, NQ):
                    row(q)

                def chunk(n, b, rb, odd, first, ahead=True):
                    if ahead:
                        transposes(n + 2, b + 2, first)
                    products(n, b, rb, odd, first)

                for b in range(GC):
                    chunk(b, b, b // NC, b // 2 + 1, True)
                with pe.Fori(1, NQ - 1) as q:
                    for b in range(GC):
                        chunk(q * GC + b, b, q * PACK + b // NC, q * (GC // 2) + b // 2 + 1, False)
                for b in range(GC):
                    chunk((NQ - 1) * GC + b, b, (NQ - 1) * PACK + b // NC, (NQ - 1) * (GC // 2) + b // 2 + 1,
                          False, ahead=b < GC - 2)
            with pe.Else():
                for q in range(2, NQ):
                    row(q)
                with pe.Fori(0, NB) as t:
                    pe.wait_ge(s["g_probs"], t + 1)
                    for q in range(NQ):
                        if q >= 4:
                            pe.wait_ge(s["g_t"], t * NQ + q - 3)
                        for r in range(PACK):
                            mm = nc.tensor.transpose(stage[:, q % 4, r * P:(r + 1) * P], expoq[:, q, r, :], ident[:])
                        mm.then_inc(s["g_tp"], 1)
                        pe.wait_ge(s["g_t"], t * NQ + q + 1)
                        for r in range(PACK):
                            mm = nc.tensor.matmul(acc[:, 0, 0:Fo], probtv[:, q % 4, r * P:(r + 1) * P],
                                                  wh[:, q * PACK + r, 0:Fo], start=(q == 0 and r == 0),
                                                  stop=(q == NQ - 1 and r == PACK - 1))
                    mm.then_inc(s["g_sums"], 1)

        @block.scalar
        def _(act):
            act.wait_ge(s["wtp_ready"], 1)
            nc.scalar.activation(wt[:], acc[:, 0, 0:P], ACT.Copy).then_inc(s["wt_ready"], 1)
            nc.scalar.activation(wa2[:], acc[:, 0, 0:P], ACT.Square,
                                 accum_out=norms[:]).then_inc(s["norms_ready"], 1)
            act.wait_ge(s["norms_ready"], 1)
            nc.scalar.activation(lim[:, 2:3], norms[:], ACT.Sqrt, scale=1.01 * D).then_inc(s["bound_ready"], 1)
            for k in range(2):
                sl = slice(k * NB // 2, (k + 1) * NB // 2)
                act.wait_ge(s["var_ready"], k + 1)
                nc.scalar.activation(small[:, 1, sl], small[:, 0, sl], ACT.Sqrt).then_inc(s["sqrt_ready"], 1)
            for q in range(NQ + 1):
                if q < NQ:
                    act.wait_ge(s["xt_ready"], q + 1)
                    nc.scalar.activation(htb[:, q * PACK:(q + 1) * PACK, :],
                                         stage[:, q % 2, :].rearrange("p (t k) -> p t k", k=P),
                                         ACT.Relu).then_inc(s["ht_ready"], 1)
                if q >= 1:
                    g = q - 1
                    act.wait_ge(s["whp_ready"], g + 1)
                    o = wh[:, g * PACK:(g + 1) * PACK, :].rearrange("p (b r) c -> p b r c", b=2)
                    i = acc[:, 2 * (g % 2):2 * (g % 2) + 2, :].rearrange("p b (r c) -> p b r c", r=2)[:, :, :, 0:WC]
                    for b in range(2):
                        mm = nc.scalar.activation(o[:, b], i[:, b], ACT.Copy)
                    mm.then_inc(s["wh_ready"], 1)
            act.wait_ge(s["flag_ready"], 1)
            fast = act.value_load(flag[0:1, 0:1], min_val=0, max_val=1)

            def row(q, **how):
                act.wait_ge(s["rowp_ready"], q + 1)
                nc.scalar.activation(f2q[:, q], acc[:, 2 + q % 2, :].rearrange("p (s k) -> p s k", k=P), ACT.Copy,
                                     **how).then_inc(s["row_ready"], 1)

            with act.If(fast):
                act.wait_ge(s["exparg_ready"], 1)
                for k, o in enumerate((us, vs, U, V)):
                    ins = nc.scalar.activation(o[:], small[:, k, :], ACT.Exp)
                ins.then_inc(s["exps_ready"], 1)

                def high_parts(k):
                    q, parts = k // 2, (negv, posv)[k % 2]
                    act.wait_ge(s["scaled_ready"], k + 1)
                    nc.scalar.activation(parts[:, q * PACK:(q + 1) * PACK, 0, 0:E1], tmp[:, k % 2],
                                         ACT.Copy, scale=1.0 / LOW).then_inc(s["high_ready"], 1)

                def odd_masks(n, b):
                    return (n - b) // 2 + b // 2 + 1

                turned = act.alloc_register("transposed_count")
                masked = act.alloc_register("masks_ready_count")

                def evacuate(n, b, looped=False):
                    if looped or n >= 3:
                        if b % 2:
                            act.wait_ge(s["act_masks"], odd_masks(n, b) - 1)
                    if looped:
                        act.wait_ge(s["transposed"], turned)
                        act.wait_ge(s["masks_ready"], masked)
                        act.reg_add(turned, turned, 1)
                        act.reg_add(masked, masked, 1)
                    else:
                        act.wait_ge(s["transposed"], n + 1)
                        if n >= 2:
                            act.wait_ge(s["masks_ready"], n - 1)
                    nc.scalar.activation(
                        codet[:, b % 2, :].rearrange("p (s w) -> p s w", s=PACK),
                        stage[:, b % 4, :].bitcast(F8).rearrange("p (w s) -> p s w", s=PACK),
                        ACT.Sign).then_inc(s["evacuated"], 1)

                def act_mask(n, b, first=False):
                    act.wait_ge(s["evacuated"], n + 1)
                    if not (first and b < 2):
                        act.wait_ge(s["masks_used"], n - 1)
                    nc.scalar.activation(mneg[:, b % 2, :], codet[:, b % 2, :], ACT.Relu, scale=-1.0
                                         ).then_inc(s["act_masks"], 1)

                def first_term(rb, parity, t):
                    act.wait_ge(s["masks_used"], (rb + 1) * NC)
                    nc.scalar.activation(num[:, parity, :], acc[:, 2 * parity, 0:E1], ACT.Copy,
                                         scale=U[:, bass.ds(t, 1)]).then_inc(s["first_term"], 1)

                for c in range(NC + 1):
                    for q in range(c * QC, (c + 1) * QC):
                        if c < NC:
                            row(q, bias=ROUND)
                        if c > 0:
                            high_parts(2 * (q - QC))
                            high_parts(2 * (q - QC) + 1)
                    if c > 0:
                        evacuate(c - 1, c - 1)
                        if c % 2 == 0:
                            act_mask(c - 1, c - 1, first=c == 2)
                for b in range(NC, GC):
                    evacuate(b, b)
                    if b % NC == 1:
                        first_term(b // NC - 1, (b // NC - 1) % 2, b // NC - 1)
                    if b % 2:
                        act_mask(b, b)
                act.reg_mov(turned, GC + 1)
                act.reg_mov(masked, GC - 1)
                with act.Fori(1, NQ) as q:
                    for b in range(GC):
                        evacuate(q * GC + b, b, looped=True)
                        if b % NC == 1:
                            first_term(q * PACK + b // NC - 1, (b // NC - 1) % 2, q * PACK + b // NC - 1)
                        if b % 2:
                            act_mask(q * GC + b, b)
                first_term(NB - 1, (NB - 1) % 2, NB - 1)
            with act.Else():
                for q in range(NQ):
                    row(q, scale=1.0 / SCORE_SCALE)
                with act.Fori(0, NB) as t:
                    act.wait_ge(s["g_shift"], t + 1)
                    nc.scalar.activation(expo, expo, ACT.Exp, bias=gm[:, 1:2],
                                         accum_out=gm[:, 2:3]).then_inc(s["g_probs"], 1)
                    for q in range(NQ):
                        act.wait_ge(s["g_tp"], t * NQ + q + 1)
                        nc.scalar.activation(probtv[:, q % 4, :], stage[:, q % 4, :], ACT.Copy).then_inc(s["g_t"], 1)

        @block.vector
        def _(dve):
            steps = [0]

            def then(ins):
                steps[0] += 1
                ins.then_inc(s["dve_step"], 1)
                dve.wait_ge(s["dve_step"], steps[0])

            me, mo = stats[:, :, 1], stats[:, :, 4]

            def statistics(h):
                for t in range(h * NB // 2, (h + 1) * NB // 2):
                    if t % (NB // 4) == 0:
                        dve.wait_ge(x_loaded[t // (NB // 4)], 16)
                    ins = nc.vector.bn_stats(stats[:, t, :], x_sb[:, t, :])
                then(ins)

            def variance(h):
                sl = slice(h * NB // 2, (h + 1) * NB // 2)
                nc.vector.tensor_tensor(small[:, 0, sl], me[:, sl], mo[:, sl], ALU.subtract)
                nc.vector.tensor_tensor(small[:, 2, sl], stats[:, sl, 2], stats[:, sl, 5], ALU.add)
                then(nc.vector.tensor_tensor(mean[:, sl], me[:, sl], mo[:, sl], ALU.add))
                nc.vector.tensor_scalar(mean[:, sl], mean[:, sl], 0.5, None, ALU.mult)
                then(nc.vector.tensor_tensor(small[:, 1, sl], small[:, 0, sl], small[:, 0, sl], ALU.mult))
                then(nc.vector.tensor_scalar(small[:, 3, sl], small[:, 1, sl], 0.25, EPS, ALU.mult, ALU.add))
                nc.vector.scalar_tensor_tensor(out=small[:, 0, sl], in0=small[:, 2, sl], scalar=1.0 / D,
                                               in1=small[:, 3, sl], op0=ALU.mult, op1=ALU.add
                                               ).then_inc(s["var_ready"], 1)

            def normalise(h):
                sl = slice(h * NB // 2, (h + 1) * NB // 2)
                dve.wait_ge(s["sqrt_ready"], h + 1)
                then(nc.vector.reciprocal(rstd[:, sl], small[:, 1, sl]))
                then(nc.vector.tensor_tensor(small[:, 2, sl], rstd[:, sl], rstd[:, sl], ALU.mult))
                then(nc.vector.tensor_tensor(small[:, 3, sl], small[:, 2, sl], small[:, 0, sl], ALU.mult))
                then(nc.vector.tensor_scalar(small[:, 2, sl], small[:, 3, sl], -0.5, 1.5, ALU.mult, ALU.add))
                then(nc.vector.tensor_tensor(rstd[:, sl], rstd[:, sl], small[:, 2, sl], ALU.mult))
                for t in range(h * NB // 2, (h + 1) * NB // 2):
                    ins = nc.vector.tensor_scalar(xn[:, t, :], x_sb[:, t, :], mean[:, t:t + 1],
                                                  rstd[:, t:t + 1], ALU.subtract, ALU.mult)
                    if t % PACK == PACK - 1:
                        ins.then_inc(s["xn_ready"], 1)

            statistics(0)
            variance(0)
            dve.wait_ge(s["wap_ready"], 1)
            dve.wait_ge(s["norms_ready"], 1)
            then(nc.vector.tensor_copy(wx[:, Fo:WC], acc[:, 1, 0:2]))
            nc.vector.tensor_scalar(wa2[:], wx[:, Fo + 1:WC].to_broadcast([P, P]), SCORE_SCALE, None,
                                    ALU.mult).then_inc(s["wx_ready"], 1)
            statistics(1)
            variance(1)
            normalise(0)
            normalise(1)
            f1, f2 = wh[:, :, Fo], wh[:, :, Fo + 1]
            dve.wait_ge(s["wh_ready"], NQ)
            nc.vector.reduce_max(lim[:, 0:1], f2, AX_X)
            then(nc.vector.tensor_reduce(low[:], f2, AX_X, ALU.min))
            nc.vector.tensor_scalar(lim[:, 1:2], low[:], -1.0, None, ALU.mult).then_inc(s["limits_ready"], 1)
            then(nc.vector.tensor_scalar(f1q[:], f1, SCORE_SCALE, None, ALU.mult))
            then(nc.vector.tensor_scalar(f1q[:], f1q[:], CLAMP, -CLAMP, ALU.min, ALU.max))
            then(nc.vector.tensor_scalar(f1q[:], f1q[:], ROUND, ROUND, ALU.add, ALU.subtract))
            then(nc.vector.tensor_scalar(f1q[:], f1q[:], HALF, None, ALU.add))
            dve.wait_ge(s["limits_reduced"], 1)
            F, nF, mW = glim[:, 0:1], glim[:, 1:2], glim[:, 2:3]
            then(nc.vector.tensor_scalar(gs[:, 0:1], F, nF, SPREAD_LIMIT, ALU.add, ALU.is_le))
            then(nc.vector.tensor_scalar(gs[:, 1:2], F, nF, F2_LIMIT, ALU.max, ALU.is_le))
            then(nc.vector.tensor_scalar(gs[:, 2:3], mW, WH_LIMITS[1], gs[:, 1:2], ALU.is_le, ALU.mult))
            then(nc.vector.tensor_scalar(gs[:, 3:4], mW, WH_LIMITS[0], gs[:, 2:3], ALU.is_ge, ALU.mult))
            nc.vector.tensor_scalar(flag[:], gs[:, 3:4], gs[:, 0:1], None, ALU.mult).then_inc(s["flag_ready"], 1)
            dve.wait_ge(s["flag_ready"], 1)
            fast = dve.value_load(flag[0:1, 0:1], min_val=0, max_val=1)
            with dve.If(fast):
                nc.vector.tensor_scalar(small[:, 0, :], f2, F, None, ALU.subtract)
                then(nc.vector.tensor_scalar(Ul[:], f1, F, None, ALU.add))
                nc.vector.tensor_scalar(small[:, 1, :], small[:, 0, :], SLOPE, None, ALU.mult)
                nc.vector.tensor_scalar(small[:, 2, :], Ul[:], 0.0, 1.0 - SLOPE, ALU.min, ALU.mult)
                nc.vector.tensor_scalar(small[:, 3, :], Ul[:], 0.0, -(1.0 - SLOPE), ALU.max, ALU.mult
                                        ).then_inc(s["exparg_ready"], 1)
                dve.wait_ge(s["exparg_ready"], 1)
                then(nc.vector.memset(wh[:, :, Fo:E1], 1.0))
                then(nc.vector.tensor_scalar(gs[:, 4:5], mW, 1.0, None, ALU.max))
                then(nc.vector.reciprocal(gs[:, 5:6], gs[:, 4:5]))
                then(nc.vector.tensor_scalar(gs[:, 6:7], gs[:, 5:6], TOP * LOW, None, ALU.mult))
                dve.wait_ge(s["exps_ready"], 1)
                nc.vector.tensor_scalar(us[:], us[:], gs[:, 6:7], None, ALU.mult)
                nc.vector.tensor_scalar(vs[:], vs[:], gs[:, 6:7], None, ALU.mult).then_inc(s["factors_ready"], 1)
                nc.vector.tensor_scalar(Ul[:], U[:], 1.0 / LOW, None, ALU.mult)
                nc.vector.tensor_scalar(Vl[:], V[:], 1.0 / LOW, None, ALU.mult)

                def low_parts(q):
                    sl = slice(q * PACK, (q + 1) * PACK)
                    for k, parts, done in ((2 * q, negv, "neg_ready"), (2 * q + 1, posv, "pos_ready")):
                        dve.wait_ge(s["high_ready"], k + 1)
                        nc.vector.scalar_tensor_tensor(out=parts[:, sl, 1, 0:E1], in0=parts[:, sl, 0, 0:E1],
                                                       scalar=-LOW, in1=tmp[:, k % 2], op0=ALU.mult,
                                                       op1=ALU.add).then_inc(s[done], 1)

                def row_chunk(c):
                    sl = slice(c * CHUNK, (c + 1) * CHUNK)
                    dve.wait_ge(s["row_ready"], (c + 1) * QC)
                    nc.vector.tensor_scalar(f2row[:, sl], f2row[:, sl], ROUND, None, ALU.subtract
                                            ).then_inc(s["row_even"], 1)

                def f1_column(t, rb):
                    nc.vector.tensor_copy(f1c[:, rb % 2:rb % 2 + 1], f1q[:, bass.ds(t, 1)]
                                          ).then_inc(s["f1_ready"], 1)

                turned = dve.alloc_register("transposed_count")

                def codes(n, b, t, first=False, last=False, final=False):
                    c, rb = b % NC, b // NC
                    dve.wait_ge(adj_loaded[c], 16 * (t + 1))
                    if first and b < NC:
                        dve.wait_ge(s["row_even"], c + 1)
                    if c == 0:
                        dve.wait_ge(s["f1_ready"], t + 1)
                    if first or last:
                        if not (first and b < 4):
                            dve.wait_ge(s["transposed"], n - 3)
                    else:
                        dve.wait_ge(s["transposed"], turned)
                        dve.reg_add(turned, turned, 1)
                    nc.vector.scalar_tensor_tensor(out=code[:, b % 4, :], in0=f2row[:, c * CHUNK:(c + 1) * CHUNK],
                                                   scalar=f1c[:, rb % 2:rb % 2 + 1], in1=adj_sb[:, c, :],
                                                   op0=ALU.add, op1=ALU.mult, saturate=False
                                                   ).then_inc(s["chunk_read"], 1)
                    if c == NC - 2 and not final:
                        f1_column(t + 1, rb + 1)

                def masks(n, b, first=False):
                    dve.wait_ge(s["evacuated"], n + 1)
                    if not first:
                        dve.wait_ge(s["masks_used"], n - 1)
                    ins = nc.vector.tensor_scalar(mpos[:, b % 2, :], codet[:, b % 2, :], 0.0, None, ALU.max)
                    if b % 2 == 0:
                        ins = nc.vector.tensor_scalar(mneg[:, b % 2, :], codet[:, b % 2, :], -1.0, 0.0,
                                                      ALU.mult, ALU.max)
                    ins.then_inc(s["masks_ready"], 1)

                def finish(step, rb, parity):
                    r, t = num[:, parity, :], rb
                    if step == 0:
                        dve.wait_ge(s["first_term"], rb + 1)
                        ins = nc.vector.scalar_tensor_tensor(out=r, in0=acc[:, 2 * parity, E1:2 * E1],
                                                             scalar=Ul[:, bass.ds(t, 1)], in1=r,
                                                             op0=ALU.mult, op1=ALU.add)
                    else:
                        dve.wait_ge(s["term_ready"], 4 * rb + step)
                    if step in (1, 2):
                        f, o = ((V, 0), (Vl, E1))[step - 1]
                        ins = nc.vector.scalar_tensor_tensor(out=r, in0=acc[:, 2 * parity + 1, o:o + E1],
                                                             scalar=f[:, bass.ds(t, 1)], in1=r,
                                                             op0=ALU.mult, op1=ALU.add)
                    if step == 3:
                        ins = nc.vector.reciprocal(inv[:, parity:parity + 1], num[:, parity, Fo:E1])
                    if step < 4:
                        ins.then_inc(s["term_ready"], 1)
                    else:
                        xt = x_sb[:, bass.ds(t, 1), :].rearrange("p o d -> p (o d)")
                        nc.vector.scalar_tensor_tensor(out=xt, in0=num[:, parity, 0:Fo],
                                                       scalar=inv[:, parity:parity + 1], in1=xt,
                                                       op0=ALU.mult, op1=ALU.add).then_inc(s["rows_done"], 1)

                def chunk(n, b, base, first=False, ahead=True, last=False):
                    rb = b // NC
                    done = not (first and rb == 0)
                    if not (first and b < 3):
                        masks(n, b)
                    if done and b % NC >= 1:
                        finish(2 * (b % NC) - 2, base + rb - 1, (rb - 1) % 2)
                    if ahead and not (first and b == 0):
                        codes(n + 3, b + 3, base + (b + 3) // NC, first, last, last and b + 3 >= GC - NC)
                    if done and 1 <= b % NC <= 2:
                        finish(2 * (b % NC) - 1, base + rb - 1, (rb - 1) % 2)

                f1_column(0, 0)
                for c in range(NC):
                    row_chunk(c)
                    codes(c, c, 0, first=True)
                    if c >= 1:
                        masks(c - 1, c - 1, first=c < 3)
                    for q in range(c * QC, (c + 1) * QC):
                        low_parts(q)
                for b in range(GC):
                    chunk(b, b, 0, first=True)
                dve.reg_mov(turned, GC)
                with dve.Fori(1, NQ - 1) as q:
                    for b in range(GC):
                        chunk(q * GC + b, b, q * PACK)
                for b in range(GC):
                    chunk((NQ - 1) * GC + b, b, (NQ - 1) * PACK, ahead=b < GC - 3, last=True)
                for st in range(5):
                    finish(st, NB - 1, (NB - 1) % 2)
            with dve.Else():
                dve.wait_ge(s["row_ready"], NQ)
                GS = 3 * NC + 5
                with dve.Fori(0, NB) as t:
                    f1t = wh[:, bass.ds(t, 1), Fo:E1].rearrange("p o c -> p (o c)")
                    for c in range(NC):
                        sl = slice(c * CHUNK, (c + 1) * CHUNK)
                        dve.wait_ge(adj_loaded[c], 16 * (t + 1))
                        nc.vector.tensor_scalar(dropv, adj_sb[:, c, :], 1.0, NEG, ALU.subtract, ALU.mult
                                                ).then_inc(s["chunk_read"], 1)
                        nc.vector.tensor_scalar(scorev, f2row[:, sl], f1t, None, ALU.add).then_inc(s["g_step"], 1)
                        dve.wait_ge(s["g_step"], t * GS + 3 * c + 1)
                        nc.vector.scalar_tensor_tensor(out=scorev, in0=scorev, scalar=SLOPE, in1=scorev,
                                                       op0=ALU.mult, op1=ALU.max).then_inc(s["g_step"], 1)
                        dve.wait_ge(s["g_step"], t * GS + 3 * c + 2)
                        dve.wait_ge(s["chunk_read"], t * NC + c + 1)
                        nc.vector.tensor_tensor(expo[:, sl], scorev, dropv, ALU.add).then_inc(s["g_step"], 1)
                        dve.wait_ge(s["g_step"], t * GS + 3 * c + 3)
                    nc.vector.reduce_max(gm[:, 0:1], expo, AX_X).then_inc(s["g_step"], 1)
                    dve.wait_ge(s["g_step"], t * GS + 3 * NC + 1)
                    nc.vector.tensor_scalar(gm[:, 1:2], gm[:, 0:1], -1.0, None, ALU.mult).then_inc(s["g_shift"], 1)
                    nc.vector.tensor_scalar(gm[:, 3:4], gm[:, 0:1], -NEG / 2, None, ALU.is_gt
                                            ).then_inc(s["g_step"], 1)
                    dve.wait_ge(s["g_step"], t * GS + 3 * NC + 2)
                    dve.wait_ge(s["g_sums"], t + 1)
                    nc.vector.tensor_tensor(gm[:, 4:5], gm[:, 2:3], gm[:, 3:4], ALU.mult).then_inc(s["g_step"], 1)
                    dve.wait_ge(s["g_step"], t * GS + 3 * NC + 3)
                    nc.vector.reciprocal(gm[:, 5:6], gm[:, 4:5]).then_inc(s["g_step"], 1)
                    nc.vector.tensor_scalar(num[:, 0, 0:Fo], acc[:, 0, 0:Fo], gm[:, 3:4], None, ALU.mult
                                            ).then_inc(s["g_step"], 1)
                    dve.wait_ge(s["g_step"], t * GS + 3 * NC + 5)
                    xt = x_sb[:, bass.ds(t, 1), :].rearrange("p o d -> p (o d)")
                    nc.vector.scalar_tensor_tensor(out=xt, in0=num[:, 0, 0:Fo], scalar=gm[:, 5:6], in1=xt,
                                                   op0=ALU.mult, op1=ALU.add).then_inc(s["rows_done"], 1)


_INS = ["x", "adj", "L0_gnn_W", "L0_gnn_a"]


def kernel(**inputs):
    import numpy as _np
    import concourse.bacc as _bacc
    from concourse import mybir as _mybir
    from concourse.bass_utils import run_bass_kernel_spmd as _run

    nc = _bacc.Bacc("TRN2", target_bir_lowering=False, num_devices=1)
    arrays, args = {}, []
    for name in _INS:
        v = _np.ascontiguousarray(inputs[name])
        arrays[f"in_{name}_dram"] = v
        args.append(nc.dram_tensor(f"in_{name}_dram", v.shape, _mybir.dt.from_np(v.dtype), kind="ExternalInput").ap())
    shape = inputs["x"].shape
    args.append(nc.dram_tensor("out_0_dram", shape, _mybir.dt.float32, kind="ExternalOutput").ap())
    gat_kernel(nc, *args)
    r = _run(nc, [arrays], core_ids=[0])
    return r.results[0]["out_0_dram"]
```

```python
from contextlib import ExitStack

import concourse.bass as bass
from concourse import mybir

ALU = mybir.AluOpType
ACT = mybir.ActivationFunctionType
AX_X = mybir.AxisListType.X
F32 = mybir.dt.float32
F16 = mybir.dt.float16
BF16 = mybir.dt.bfloat16
F8 = mybir.dt.float8e5
I32 = mybir.dt.int32

P = 128
PACK = 4
BANK = 512
CHUNK = PACK * BANK
SLOPE = 0.2
EPS = 1e-5
LOW = 2048.0
TOP = 16384.0
NEG = 3.0e38
SCORE_SCALE = 256.0
ROUND = 12288.0
HALF = 2.0 ** -11
CLAMP = 4000.0
F2_LIMIT = 15.0
SPREAD_LIMIT = 14.0
WH_LIMITS = (2.0 ** -8, 2.0 ** 6)


def gat_kernel(nc, x, adj, W, a, out):
    N, D = x.shape
    Fo = W.shape[1]
    NB = N // P
    NQ = NB // PACK
    NC = N // CHUNK
    QC = CHUNK // (P * PACK)
    GC = PACK * NC
    TMP = 4
    NX = 4
    E1 = Fo + 1
    WC = Fo + 2
    assert D == P and Fo == P and N % CHUNK == 0 and 2 * WC * 2 == WC * 4

    with ExitStack() as ctx:
        def sb(name, shape, dt):
            return ctx.enter_context(nc.sbuf_tensor(name, shape, dt))

        def ps(name, shape, dt):
            return ctx.enter_context(nc.psum_tensor(name, shape, dt))

        def sem(name):
            return ctx.enter_context(nc.semaphore(name))

        x_sb = sb("x_sb", [P, NB, D], F32)
        wh = sb("wh", [P, NB, WC], F32)
        pos = wh.bitcast(F16)
        ht = sb("ht", [P, NB, WC], F32)
        neg = ht.bitcast(F16)
        f2row = sb("f2row", [P, N], F32)
        adj_sb = sb("adj_sb", [P, NC, CHUNK], I32)
        code = sb("code", [P, 4, CHUNK], F8)
        codet = sb("codet", [P, 2, CHUNK], BF16)
        mpos = sb("mpos", [P, 2, CHUNK], F16)
        mneg = sb("mneg", [P, 2, CHUNK], F16)
        ident = sb("ident", [P, P], F32)
        wx = sb("wx", [P, WC], F32)
        wt = sb("wt", [P, P], F32)
        a_sb = sb("a_sb", [P, 2], F32)
        mean = sb("mean", [P, NB], F32)
        rstd = sb("rstd", [P, NB], F32)
        small = sb("small", [P, 4, NB], F32)
        low = sb("low", [P, 1], F32)
        norms = sb("norms", [P, 1], F32)
        lim = sb("lim", [P, 3], F32)
        glim = sb("glim", [P, 3], F32)
        gs = sb("gs", [P, 8], F32)
        flag = sb("flag", [P, 1], I32)
        f1q = sb("f1q", [P, NB], F32)
        f1c = sb("f1c", [P, 2], F32)
        vu = sb("vu", [P, 2, NB], F32)
        U = sb("U", [P, NB], F32)
        V = sb("V", [P, NB], F32)
        Ul = sb("Ul", [P, NB], F32)
        Vl = sb("Vl", [P, NB], F32)
        num = sb("num", [P, 2, E1], F32)
        inv = sb("inv", [P, 2], F32)
        tmp = sb("tmp", [P, TMP, PACK, E1], F32)
        gm = sb("gm", [P, 6], F32)
        drop = mpos.bitcast(F32)
        score = mneg.bitcast(F32)
        probt = codet.bitcast(F32)

        acc = ps("acc", [P, 4, BANK], F32)
        stage = ps("stage", [P, 4, BANK], F32)

        s = {n: sem(n) for n in (
            "x_loaded0", "x_loaded1", "x_loaded2", "x_loaded3", "w_loaded", "a_loaded",
            "adj_loaded0", "adj_loaded1", "adj_loaded2", "adj_loaded3",
            "ident_zero", "ident_ready", "chunk_read", "rows_done", "out_stored",
            "dve_step", "limits_ready", "limits_reduced", "flag_ready",
            "sqrt_ready", "var_ready", "rstd_ready", "xn_ready", "centred", "xn_late_ready", "xt_ready",
            "ht_ready", "whp_ready", "wh_ready", "rowp_ready", "row_ready", "row_even",
            "wtp_ready", "wt_ready", "wap_ready", "wx_ready", "norms_ready", "bound_ready",
            "exparg_ready", "exps_ready", "factors_ready", "scaled_ready", "high_ready", "pos_ready", "neg_ready",
            "f1_ready", "transposed", "evacuated", "masks_ready", "act_masks", "masks_used", "first_term",
            "term_ready", "g_step", "g_shift", "g_probs", "g_tp", "g_t", "g_sums")}
        adj_loaded = [s[f"adj_loaded{c}"] for c in range(NC)]
        x_loaded = [s[f"x_loaded{c}"] for c in range(NX)]

        x_dram = x.rearrange("(q p s) d -> p q (s d)", p=P, s=PACK)
        out_dram = out.rearrange("(q p s) d -> p q (s d)", p=P, s=PACK)
        adj_dram = adj.rearrange("(q p s) (c k) -> q s c p k", p=P, s=PACK, k=CHUNK)
        xq = x_sb[:].rearrange("p (q s) d -> p q (s d)", s=PACK)
        XP = NQ // NX

        def dve_has(g):
            return g % XP == 0 or g == NQ - XP + 1

        def dve_groups(g):
            return sum(dve_has(k) for k in range(g + 1))

        htb = ht[:].rearrange("p t c -> p (t c)")[:, 0:N].rearrange("p (t k) -> p t k", k=P)
        xn = wh[:].rearrange("p t c -> p (t c)")[:, 0:N].rearrange("p (t k) -> p t k", k=P)
        squares = f2row[:, 0:P]
        stats = f2row[:, P:P + 6 * NB].rearrange("p (t k) -> p t k", k=6)
        f2q = f2row[:].rearrange("p (q k s) -> p q s k", k=P, s=PACK)
        dropv = drop[:].rearrange("p a b -> p (a b)")
        scorev = score[:].rearrange("p a b -> p (a b)")
        probtv = probt[:].rearrange("p a (b c) -> p (a b) c", c=BANK)
        expo = htb.rearrange("p t k -> p (t k)")
        expoq = expo.rearrange("p (q k s) -> p q s k", k=P, s=PACK)
        posv = pos[:].rearrange("p t (h c) -> p t h c", h=2)
        negv = neg[:].rearrange("p t (h c) -> p t h c", h=2)

        block = ctx.enter_context(nc.Block())

        @block.sync
        def _(sp):
            for k in range(2):
                sp.dma_start(xq[:, k * XP:(k + 1) * XP, :],
                             x_dram[:, k * XP:(k + 1) * XP, :]).then_inc(x_loaded[k], 16)
            sp.dma_start(wx[:, 0:Fo], W).then_inc(s["w_loaded"], 16)
            with nc.allow_non_contiguous_dma(reason="the 256 values of a, once"):
                sp.dma_start(a_sb[:], a.rearrange("(c f) o -> f (c o)", c=2)).then_inc(s["a_loaded"], 16)
            for k in range(2, NX):
                sp.dma_start(xq[:, k * XP:(k + 1) * XP, :],
                             x_dram[:, k * XP:(k + 1) * XP, :]).then_inc(x_loaded[k], 16)

            def load(q, r, c):
                sp.dma_start(adj_sb[:, c, :], adj_dram[q, r, c]).then_inc(adj_loaded[c], 16)

            for c in range(NC):
                load(0, 0, c)
            for r in range(1, PACK):
                for c in range(NC):
                    sp.wait_ge(s["chunk_read"], (r - 1) * NC + c + 1)
                    load(0, r, c)
            with sp.Fori(1, NQ) as q:
                for r in range(PACK):
                    for c in range(NC):
                        sp.wait_ge(s["chunk_read"], q * GC + (r - 1) * NC + c + 1)
                        load(q, r, c)
                    if r == 1:
                        sp.wait_ge(s["rows_done"], q * PACK)
                        sp.dma_start(out_dram[:, q - 1, :], xq[:, q - 1, :]).then_inc(s["out_stored"], 16)
            sp.wait_ge(s["rows_done"], NB)
            sp.dma_start(out_dram[:, NQ - 1, :], xq[:, NQ - 1, :]).then_inc(s["out_stored"], 16)
            sp.wait_ge(s["out_stored"], 16 * NQ)

        @block.gpsimd
        def _(pool):
            nc.gpsimd.memset(ident[:], 0.0).then_inc(s["ident_zero"], 1)
            pool.wait_ge(s["ident_zero"], 1)
            nc.gpsimd.affine_select(out=ident[:], in_=ident[:], compare_op=ALU.not_equal, fill=1.0, base=0,
                                    pattern=[[-1, P]], channel_multiplier=1).then_inc(s["ident_ready"], 1)
            for g in range(NQ):
                k, sl = g // XP, slice(g * PACK, (g + 1) * PACK)
                if dve_has(g):
                    continue
                pool.wait_ge(s["rstd_ready"], k + 1)
                nc.gpsimd.tensor_tensor(xn[:, sl, :], x_sb[:, sl, :],
                                        mean[:, sl].unsqueeze(2).to_broadcast([P, PACK, D]),
                                        ALU.subtract).then_inc(s["centred"], 1)
                pool.wait_ge(s["centred"], g + 1 - dve_groups(g))
                nc.gpsimd.tensor_tensor(xn[:, sl, :], xn[:, sl, :],
                                        rstd[:, sl].unsqueeze(2).to_broadcast([P, PACK, D]),
                                        ALU.mult).then_inc(s["xn_late_ready"], 1)
            pool.wait_ge(s["limits_ready"], 1)
            pool.wait_ge(s["bound_ready"], 1)
            nc.gpsimd.partition_all_reduce(glim[:], lim[:], P,
                                           bass.bass_isa.ReduceOp.max).then_inc(s["limits_reduced"], 1)
            pool.wait_ge(s["flag_ready"], 1)
            fast = pool.value_load(flag[0:1, 0:1], min_val=0, max_val=1)
            with pool.If(fast):
                pool.wait_ge(s["factors_ready"], 1)
                for q in range(NQ):
                    sl, h = slice(q * PACK, (q + 1) * PACK), q * 2 % TMP
                    if 2 * q >= TMP:
                        pool.wait_ge(s["pos_ready"], q - TMP // 2 + 1)
                    nc.gpsimd.tensor_tensor(tmp[:, h:h + 2],
                                            wh[:, sl, 0:E1].unsqueeze(1).to_broadcast([P, 2, PACK, E1]),
                                            vu[:, :, sl].unsqueeze(3).to_broadcast([P, 2, PACK, E1]),
                                            ALU.mult).then_inc(s["scaled_ready"], 1)
            with pool.Else():
                pass

        @block.tensor
        def _(pe):
            pe.wait_ge(s["ident_ready"], 1)
            pe.wait_ge(s["w_loaded"], 16)
            nc.tensor.transpose(acc[:, 0, 0:P], wx[:, 0:Fo], ident[:]).then_inc(s["wtp_ready"], 1)
            pe.wait_ge(s["wt_ready"], 1)
            pe.wait_ge(s["a_loaded"], 16)
            nc.tensor.matmul(acc[:, 1, 0:2], wt[:], a_sb[:], start=True, stop=True).then_inc(s["wap_ready"], 1)
            for q in range(NQ + 1):
                if q < NQ:
                    if dve_has(q):
                        pe.wait_ge(s["xn_ready"], dve_groups(q))
                    else:
                        pe.wait_ge(s["xn_late_ready"], q + 1 - dve_groups(q))
                    if q >= 2:
                        pe.wait_ge(s["ht_ready"], q - 1)
                    for r in range(PACK):
                        mm = nc.tensor.transpose(stage[:, q % 2, r * P:(r + 1) * P], xn[:, q * PACK + r, :],
                                                 ident[:])
                    mm.then_inc(s["xt_ready"], 1)
                if q >= 1:
                    g = q - 1
                    if g == 0:
                        pe.wait_ge(s["wx_ready"], 1)
                    pe.wait_ge(s["ht_ready"], g + 1)
                    if g >= 2:
                        pe.wait_ge(s["wh_ready"], g - 1)
                    for r in range(PACK):
                        o = acc[:, 2 * (g % 2) + r // 2, (r % 2) * 256:(r % 2) * 256 + WC]
                        mm = nc.tensor.matmul(o, htb[:, g * PACK + r, :], wx[:], start=(r % 2 == 0),
                                              stop=(r % 2 == 1), skip_group_check=True)
                    mm.then_inc(s["whp_ready"], 1)

            def row(q, n):
                if n >= 4:
                    pe.wait_ge(s["row_ready"], n - 3)
                for r in range(PACK):
                    mm = nc.tensor.transpose(acc[:, n % 4, r * P:(r + 1) * P],
                                             wh[:, q * PACK + r, Fo + 1:WC].to_broadcast([P, P]), ident[:])
                mm.then_inc(s["rowp_ready"], 1)

            pe.wait_ge(s["wh_ready"], NQ)
            for q in range(NQ // 2):
                row(q, q)
            pe.wait_ge(s["flag_ready"], 1)
            fast = pe.value_load(flag[0:1, 0:1], min_val=0, max_val=1)

            def transposes(n, b, first=False):
                pe.wait_ge(s["chunk_read"], n + 1)
                if not (first and b < 4):
                    pe.wait_ge(s["evacuated"], n - 3)
                for k in range(QC):
                    mm = nc.tensor.transpose(stage[:, b % 4, k * P:(k + 1) * P],
                                             code[:, b % 4, :].bitcast(F32)[:, k * P:(k + 1) * P], ident[:])
                mm.then_inc(s["transposed"], 1)

            def products(n, b, rb, odd, first=False, turn=None):
                pe.wait_ge(s["masks_ready"], n + 1)
                if b % 2:
                    pe.wait_ge(s["act_masks"], odd)
                c, parity = b % NC, (b // NC) % 2
                if first and b == 0:
                    pe.wait_ge(s["row_ready"], NQ)
                if c == 0 and not (first and b < 2 * NC):
                    pe.wait_ge(s["rows_done"], rb - 1)
                for k in range(QC):
                    if first and k == QC // 2:
                        transposes(turn, turn, first=True)
                    for r in range(PACK):
                        t = (c * QC + k) * PACK + r
                        w = slice((r * QC + k) * P, (r * QC + k + 1) * P)
                        if first and rb == 0 and r == 0:
                            pe.wait_ge(s["neg_ready"], c * QC + k + 1)
                            pe.wait_ge(s["pos_ready"], c * QC + k + 1)
                        st, sp_ = (c == 0 and k == 0 and r == 0), (c == NC - 1 and k == QC - 1 and r == PACK - 1)
                        nc.tensor.matmul(acc[:, 2 * parity, 0:2 * E1], mpos[:, b % 2, w], posv[:, t, :, 0:E1],
                                         start=st, stop=sp_)
                        mm = nc.tensor.matmul(acc[:, 2 * parity + 1, 0:2 * E1], mneg[:, b % 2, w],
                                              negv[:, t, :, 0:E1], start=st, stop=sp_)
                mm.then_inc(s["masks_used"], 1)

            with pe.If(fast):
                for q in range(NQ // 2, NQ):
                    if q == NQ - QC:
                        transposes(0, 0, first=True)
                    row(q, q)
                for b in range(GC):
                    if b == NC - 1:
                        transposes(NC, NC, first=True)
                    products(b, b, b // NC, b // 2 + 1, first=True, turn=b + (1 if b < NC - 1 else 2))
                with pe.Fori(1, NQ - 1) as q:
                    for b in range(GC):
                        transposes(q * GC + b + 2, b + 2)
                        products(q * GC + b, b, q * PACK + b // NC, q * (GC // 2) + b // 2 + 1)
                for b in range(GC):
                    if b < GC - 2:
                        transposes((NQ - 1) * GC + b + 2, b + 2)
                    products((NQ - 1) * GC + b, b, (NQ - 1) * PACK + b // NC, (NQ - 1) * (GC // 2) + b // 2 + 1)
            with pe.Else():
                for q in range(NQ):
                    row(q, NQ // 2 + q)
                with pe.Fori(0, NB) as t:
                    pe.wait_ge(s["g_probs"], t + 1)
                    for q in range(NQ):
                        if q >= 4:
                            pe.wait_ge(s["g_t"], t * NQ + q - 3)
                        for r in range(PACK):
                            mm = nc.tensor.transpose(stage[:, q % 4, r * P:(r + 1) * P], expoq[:, q, r, :], ident[:])
                        mm.then_inc(s["g_tp"], 1)
                        pe.wait_ge(s["g_t"], t * NQ + q + 1)
                        for r in range(PACK):
                            mm = nc.tensor.matmul(acc[:, 0, 0:Fo], probtv[:, q % 4, r * P:(r + 1) * P],
                                                  wh[:, q * PACK + r, 0:Fo], start=(q == 0 and r == 0),
                                                  stop=(q == NQ - 1 and r == PACK - 1))
                    mm.then_inc(s["g_sums"], 1)

        @block.scalar
        def _(act):
            act.wait_ge(s["wtp_ready"], 1)
            nc.scalar.activation(wt[:], acc[:, 0, 0:P], ACT.Copy).then_inc(s["wt_ready"], 1)
            nc.scalar.activation(squares, acc[:, 0, 0:P], ACT.Square,
                                 accum_out=norms[:]).then_inc(s["norms_ready"], 1)
            act.wait_ge(s["norms_ready"], 1)
            nc.scalar.activation(lim[:, 2:3], norms[:], ACT.Sqrt, scale=1.01 * D).then_inc(s["bound_ready"], 1)

            def root(k):
                sl = slice(k * NB // NX, (k + 1) * NB // NX)
                act.wait_ge(s["var_ready"], k + 1)
                nc.scalar.activation(small[:, 1, sl], small[:, 0, sl], ACT.Sqrt).then_inc(s["sqrt_ready"], 1)

            root(0)
            for q in range(NQ + 1):
                if q % XP == 2 and q // XP + 1 < NX:
                    root(q // XP + 1)
                if q < NQ:
                    act.wait_ge(s["xt_ready"], q + 1)
                    nc.scalar.activation(htb[:, q * PACK:(q + 1) * PACK, :],
                                         stage[:, q % 2, :].rearrange("p (t k) -> p t k", k=P),
                                         ACT.Relu).then_inc(s["ht_ready"], 1)
                if q >= 1:
                    g = q - 1
                    act.wait_ge(s["whp_ready"], g + 1)
                    o = wh[:, g * PACK:(g + 1) * PACK, :].rearrange("p (b r) c -> p b r c", b=2)
                    i = acc[:, 2 * (g % 2):2 * (g % 2) + 2, :].rearrange("p b (r c) -> p b r c", r=2)[:, :, :, 0:WC]
                    for b in range(2):
                        mm = nc.scalar.activation(o[:, b], i[:, b], ACT.Copy)
                    mm.then_inc(s["wh_ready"], 1)

            def row(q, n, **how):
                act.wait_ge(s["rowp_ready"], n + 1)
                nc.scalar.activation(f2q[:, q], acc[:, n % 4, :].rearrange("p (s k) -> p s k", k=P), ACT.Copy,
                                     **how).then_inc(s["row_ready"], 1)

            for q in range(NQ // 2):
                row(q, q, scale=SCORE_SCALE, bias=ROUND)
            act.wait_ge(s["flag_ready"], 1)
            fast = act.value_load(flag[0:1, 0:1], min_val=0, max_val=1)

            with act.If(fast):
                act.wait_ge(s["exparg_ready"], 1)
                for k, o in enumerate((vu[:, 1], vu[:, 0], U[:], V[:])):
                    ins = nc.scalar.activation(o, small[:, k, :], ACT.Exp)
                ins.then_inc(s["exps_ready"], 1)

                def high_parts(k):
                    q, parts = k // 2, (negv, posv)[k % 2]
                    act.wait_ge(s["scaled_ready"], k // 2 + 1)
                    nc.scalar.activation(parts[:, q * PACK:(q + 1) * PACK, 0, 0:E1], tmp[:, k % TMP],
                                         ACT.Copy, scale=1.0 / LOW).then_inc(s["high_ready"], 1)

                def odd_masks(n, b):
                    return (n - b) // 2 + b // 2 + 1

                turned = act.alloc_register("transposed_count")
                masked = act.alloc_register("masks_ready_count")

                def evacuate(n, b, looped=False):
                    if looped or n >= 3:
                        if b % 2:
                            act.wait_ge(s["act_masks"], odd_masks(n, b) - 1)
                    if looped:
                        act.wait_ge(s["transposed"], turned)
                        act.wait_ge(s["masks_ready"], masked)
                        act.reg_add(turned, turned, 1)
                        act.reg_add(masked, masked, 1)
                    else:
                        act.wait_ge(s["transposed"], n + 1)
                        if n >= 2:
                            act.wait_ge(s["masks_ready"], n - 1)
                    nc.scalar.activation(
                        codet[:, b % 2, :].rearrange("p (s w) -> p s w", s=PACK),
                        stage[:, b % 4, :].bitcast(F8).rearrange("p (w s) -> p s w", s=PACK),
                        ACT.Sign).then_inc(s["evacuated"], 1)

                def act_mask(n, b, first=False):
                    act.wait_ge(s["evacuated"], n + 1)
                    if not (first and b < 2):
                        act.wait_ge(s["masks_used"], n - 1)
                    nc.scalar.activation(mneg[:, b % 2, :], codet[:, b % 2, :], ACT.Relu, scale=-1.0
                                         ).then_inc(s["act_masks"], 1)

                def first_term(rb, parity, t):
                    act.wait_ge(s["masks_used"], (rb + 1) * NC)
                    nc.scalar.activation(num[:, parity, :], acc[:, 2 * parity, 0:E1], ACT.Copy,
                                         scale=U[:, bass.ds(t, 1)]).then_inc(s["first_term"], 1)

                for c in range(NC):
                    for q in range(c * QC, (c + 1) * QC):
                        if q == c * QC + QC // 2:
                            evacuate(c, c)
                        if q < NQ // 4:
                            for k in (NQ // 2 + 2 * q, NQ // 2 + 2 * q + 1):
                                row(k, k, scale=SCORE_SCALE, bias=ROUND)
                        high_parts(2 * q)
                        high_parts(2 * q + 1)
                    if c % 2:
                        act_mask(c, c, first=c < 2)
                for b in range(NC, GC):
                    evacuate(b, b)
                    if b % NC == 1:
                        first_term(b // NC - 1, (b // NC - 1) % 2, b // NC - 1)
                    if b % 2:
                        act_mask(b, b)
                act.reg_mov(turned, GC + 1)
                act.reg_mov(masked, GC - 1)
                with act.Fori(1, NQ) as q:
                    for b in range(GC):
                        evacuate(q * GC + b, b, looped=True)
                        if b % NC == 1:
                            first_term(q * PACK + b // NC - 1, (b // NC - 1) % 2, q * PACK + b // NC - 1)
                        if b % 2:
                            act_mask(q * GC + b, b)
                first_term(NB - 1, (NB - 1) % 2, NB - 1)
            with act.Else():
                for q in range(NQ):
                    row(q, NQ // 2 + q)
                with act.Fori(0, NB) as t:
                    act.wait_ge(s["g_shift"], t + 1)
                    nc.scalar.activation(expo, expo, ACT.Exp, bias=gm[:, 1:2],
                                         accum_out=gm[:, 2:3]).then_inc(s["g_probs"], 1)
                    for q in range(NQ):
                        act.wait_ge(s["g_tp"], t * NQ + q + 1)
                        nc.scalar.activation(probtv[:, q % 4, :], stage[:, q % 4, :], ACT.Copy).then_inc(s["g_t"], 1)

        @block.vector
        def _(dve):
            steps = [0]

            def then(ins):
                steps[0] += 1
                ins.then_inc(s["dve_step"], 1)
                dve.wait_ge(s["dve_step"], steps[0])

            me, mo = stats[:, :, 1], stats[:, :, 4]

            def statistics(h):
                dve.wait_ge(x_loaded[h], 16)
                for t in range(h * NB // NX, (h + 1) * NB // NX):
                    ins = nc.vector.bn_stats(stats[:, t, :], x_sb[:, t, :])
                then(ins)

            def variance(h):
                sl = slice(h * NB // NX, (h + 1) * NB // NX)
                nc.vector.tensor_tensor(small[:, 0, sl], me[:, sl], mo[:, sl], ALU.subtract)
                nc.vector.tensor_tensor(small[:, 2, sl], stats[:, sl, 2], stats[:, sl, 5], ALU.add)
                then(nc.vector.tensor_tensor(mean[:, sl], me[:, sl], mo[:, sl], ALU.add))
                nc.vector.tensor_scalar(mean[:, sl], mean[:, sl], 0.5, None, ALU.mult)
                then(nc.vector.tensor_tensor(small[:, 1, sl], small[:, 0, sl], small[:, 0, sl], ALU.mult))
                then(nc.vector.tensor_scalar(small[:, 3, sl], small[:, 1, sl], 0.25, EPS, ALU.mult, ALU.add))
                nc.vector.scalar_tensor_tensor(out=small[:, 0, sl], in0=small[:, 2, sl], scalar=1.0 / D,
                                               in1=small[:, 3, sl], op0=ALU.mult, op1=ALU.add
                                               ).then_inc(s["var_ready"], 1)

            def normalise(h):
                sl = slice(h * NB // NX, (h + 1) * NB // NX)
                dve.wait_ge(s["sqrt_ready"], h + 1)
                then(nc.vector.reciprocal(rstd[:, sl], small[:, 1, sl]))
                then(nc.vector.tensor_tensor(small[:, 2, sl], rstd[:, sl], rstd[:, sl], ALU.mult))
                then(nc.vector.tensor_tensor(small[:, 3, sl], small[:, 2, sl], small[:, 0, sl], ALU.mult))
                then(nc.vector.tensor_scalar(small[:, 2, sl], small[:, 3, sl], -0.5, 1.5, ALU.mult, ALU.add))
                nc.vector.tensor_tensor(rstd[:, sl], rstd[:, sl], small[:, 2, sl], ALU.mult
                                        ).then_inc(s["rstd_ready"], 1)
                dve.wait_ge(s["rstd_ready"], h + 1)
                for t in [t for t in range(h * NB // NX, (h + 1) * NB // NX) if dve_has(t // PACK)]:
                    ins = nc.vector.tensor_scalar(xn[:, t, :], x_sb[:, t, :], mean[:, t:t + 1],
                                                  rstd[:, t:t + 1], ALU.subtract, ALU.mult)
                    if t % PACK == PACK - 1:
                        ins.then_inc(s["xn_ready"], 1)

            for h in range(NX):
                statistics(h)
                variance(h)
                normalise(h)
                if h == 0:
                    dve.wait_ge(s["wap_ready"], 1)
                    nc.vector.tensor_copy(wx[:, Fo:WC], acc[:, 1, 0:2]).then_inc(s["wx_ready"], 1)
            f1, f2 = wh[:, :, Fo], wh[:, :, Fo + 1]
            dve.wait_ge(s["wh_ready"], NQ)
            nc.vector.reduce_max(lim[:, 0:1], f2, AX_X)
            then(nc.vector.tensor_reduce(low[:], f2, AX_X, ALU.min))
            nc.vector.tensor_scalar(lim[:, 1:2], low[:], -1.0, None, ALU.mult).then_inc(s["limits_ready"], 1)
            then(nc.vector.tensor_scalar(f1q[:], f1, SCORE_SCALE, None, ALU.mult))
            then(nc.vector.tensor_scalar(f1q[:], f1q[:], CLAMP, -CLAMP, ALU.min, ALU.max))
            then(nc.vector.tensor_scalar(f1q[:], f1q[:], ROUND, ROUND, ALU.add, ALU.subtract))
            then(nc.vector.tensor_scalar(f1q[:], f1q[:], HALF, None, ALU.add))
            dve.wait_ge(s["limits_reduced"], 1)
            F, nF, mW = glim[:, 0:1], glim[:, 1:2], glim[:, 2:3]
            then(nc.vector.tensor_scalar(gs[:, 0:1], F, nF, SPREAD_LIMIT, ALU.add, ALU.is_le))
            then(nc.vector.tensor_scalar(gs[:, 1:2], F, nF, F2_LIMIT, ALU.max, ALU.is_le))
            then(nc.vector.tensor_scalar(gs[:, 2:3], mW, WH_LIMITS[1], gs[:, 1:2], ALU.is_le, ALU.mult))
            then(nc.vector.tensor_scalar(gs[:, 3:4], mW, WH_LIMITS[0], gs[:, 2:3], ALU.is_ge, ALU.mult))
            nc.vector.tensor_scalar(flag[:], gs[:, 3:4], gs[:, 0:1], None, ALU.mult).then_inc(s["flag_ready"], 1)
            dve.wait_ge(s["flag_ready"], 1)
            fast = dve.value_load(flag[0:1, 0:1], min_val=0, max_val=1)
            with dve.If(fast):
                def row_chunk(c):
                    sl = slice(c * CHUNK, (c + 1) * CHUNK)
                    dve.wait_ge(s["row_ready"], (c + 1) * QC)
                    nc.vector.tensor_scalar(f2row[:, sl], f2row[:, sl], ROUND, None, ALU.subtract
                                            ).then_inc(s["row_even"], 1)

                def f1_column(t, rb):
                    nc.vector.tensor_copy(f1c[:, rb % 2:rb % 2 + 1], f1q[:, bass.ds(t, 1)]
                                          ).then_inc(s["f1_ready"], 1)

                nc.vector.tensor_scalar(small[:, 0, :], f2, F, None, ALU.subtract)
                then(nc.vector.tensor_scalar(Ul[:], f1, F, None, ALU.add))
                nc.vector.tensor_scalar(small[:, 1, :], small[:, 0, :], SLOPE, None, ALU.mult)
                nc.vector.tensor_scalar(small[:, 2, :], Ul[:], 0.0, 1.0 - SLOPE, ALU.min, ALU.mult)
                nc.vector.tensor_scalar(small[:, 3, :], Ul[:], 0.0, -(1.0 - SLOPE), ALU.max, ALU.mult
                                        ).then_inc(s["exparg_ready"], 1)
                dve.wait_ge(s["exparg_ready"], 1)
                then(nc.vector.memset(wh[:, :, Fo:E1], 1.0))
                then(nc.vector.tensor_scalar(gs[:, 4:5], mW, 1.0, None, ALU.max))
                then(nc.vector.reciprocal(gs[:, 5:6], gs[:, 4:5]))
                then(nc.vector.tensor_scalar(gs[:, 6:7], gs[:, 5:6], TOP * LOW, None, ALU.mult))
                row_chunk(0)
                f1_column(0, 0)
                dve.wait_ge(s["exps_ready"], 1)
                nc.vector.tensor_scalar(vu[:], vu[:], gs[:, 6:7], None, ALU.mult).then_inc(s["factors_ready"], 1)
                nc.vector.tensor_scalar(Ul[:], U[:], 1.0 / LOW, None, ALU.mult)
                nc.vector.tensor_scalar(Vl[:], V[:], 1.0 / LOW, None, ALU.mult)

                def low_parts(q):
                    sl = slice(q * PACK, (q + 1) * PACK)
                    for k, parts, done in ((2 * q, negv, "neg_ready"), (2 * q + 1, posv, "pos_ready")):
                        dve.wait_ge(s["high_ready"], k + 1)
                        nc.vector.scalar_tensor_tensor(out=parts[:, sl, 1, 0:E1], in0=parts[:, sl, 0, 0:E1],
                                                       scalar=-LOW, in1=tmp[:, k % TMP], op0=ALU.mult,
                                                       op1=ALU.add).then_inc(s[done], 1)

                turned = dve.alloc_register("transposed_count")

                def codes(n, b, t, first=False, last=False, final=False):
                    c, rb = b % NC, b // NC
                    dve.wait_ge(adj_loaded[c], 16 * (t + 1))
                    if first and b < NC:
                        dve.wait_ge(s["row_even"], c + 1)
                    if c == 0:
                        dve.wait_ge(s["f1_ready"], t + 1)
                    if first or last:
                        if not (first and b < 4):
                            dve.wait_ge(s["transposed"], n - 3)
                    else:
                        dve.wait_ge(s["transposed"], turned)
                        dve.reg_add(turned, turned, 1)
                    nc.vector.scalar_tensor_tensor(out=code[:, b % 4, :], in0=f2row[:, c * CHUNK:(c + 1) * CHUNK],
                                                   scalar=f1c[:, rb % 2:rb % 2 + 1], in1=adj_sb[:, c, :],
                                                   op0=ALU.add, op1=ALU.mult, saturate=False
                                                   ).then_inc(s["chunk_read"], 1)
                    if c == NC - 2 and not final:
                        f1_column(t + 1, rb + 1)

                def masks(n, b, first=False):
                    dve.wait_ge(s["evacuated"], n + 1)
                    if not first:
                        dve.wait_ge(s["masks_used"], n - 1)
                    ins = nc.vector.tensor_scalar(mpos[:, b % 2, :], codet[:, b % 2, :], 0.0, None, ALU.max)
                    if b % 2 == 0:
                        ins = nc.vector.tensor_scalar(mneg[:, b % 2, :], codet[:, b % 2, :], -1.0, 0.0,
                                                      ALU.mult, ALU.max)
                    ins.then_inc(s["masks_ready"], 1)

                def finish(step, rb, parity):
                    r, t = num[:, parity, :], rb
                    if step == 0:
                        dve.wait_ge(s["first_term"], rb + 1)
                        ins = nc.vector.scalar_tensor_tensor(out=r, in0=acc[:, 2 * parity, E1:2 * E1],
                                                             scalar=Ul[:, bass.ds(t, 1)], in1=r,
                                                             op0=ALU.mult, op1=ALU.add)
                    else:
                        dve.wait_ge(s["term_ready"], 4 * rb + step)
                    if step in (1, 2):
                        f, o = ((V, 0), (Vl, E1))[step - 1]
                        ins = nc.vector.scalar_tensor_tensor(out=r, in0=acc[:, 2 * parity + 1, o:o + E1],
                                                             scalar=f[:, bass.ds(t, 1)], in1=r,
                                                             op0=ALU.mult, op1=ALU.add)
                    if step == 3:
                        ins = nc.vector.reciprocal(inv[:, parity:parity + 1], num[:, parity, Fo:E1])
                    if step < 4:
                        ins.then_inc(s["term_ready"], 1)
                    else:
                        xt = x_sb[:, bass.ds(t, 1), :].rearrange("p o d -> p (o d)")
                        nc.vector.scalar_tensor_tensor(out=xt, in0=num[:, parity, 0:Fo],
                                                       scalar=inv[:, parity:parity + 1], in1=xt,
                                                       op0=ALU.mult, op1=ALU.add).then_inc(s["rows_done"], 1)

                def chunk(n, b, base, first=False, ahead=True, last=False, lead=3):
                    rb = b // NC
                    masks(n, b)
                    if b % NC >= 1:
                        finish(2 * (b % NC) - 2, base + rb - 1, (rb - 1) % 2)
                    if ahead:
                        codes(n + lead, b + lead, base + (b + lead) // NC, first, last, last and b + lead >= GC - NC)
                    if 1 <= b % NC <= 2:
                        finish(2 * (b % NC) - 1, base + rb - 1, (rb - 1) % 2)

                for c in range(NC):
                    codes(c, c, 0, first=True)
                    for q in range(c * QC, (c + 1) * QC):
                        if q == c * QC + 1 and c < NC - 1:
                            row_chunk(c + 1)
                        if q == c * QC + 2 and c == NC - 1:
                            codes(NC, NC, 1, first=True)
                        if q == c * QC + QC - 1:
                            masks(c, c, first=c < 2)
                        low_parts(q)
                codes(NC + 1, NC + 1, 1, first=True)
                for b in range(NC, GC):
                    chunk(b, b, 0, first=True, lead=2 if b < 2 * NC else 3)
                    if b == 2 * NC - 1:
                        codes(b + 3, b + 3, (b + 3) // NC, first=True)
                dve.reg_mov(turned, GC)
                with dve.Fori(1, NQ - 1) as q:
                    for b in range(GC):
                        chunk(q * GC + b, b, q * PACK)
                for b in range(GC):
                    chunk((NQ - 1) * GC + b, b, (NQ - 1) * PACK, ahead=b < GC - 3, last=True)
                for st in range(5):
                    finish(st, NB - 1, (NB - 1) % 2)
            with dve.Else():
                dve.wait_ge(s["row_ready"], NQ // 2 + NQ)
                GS = 3 * NC + 5
                with dve.Fori(0, NB) as t:
                    f1t = wh[:, bass.ds(t, 1), Fo:E1].rearrange("p o c -> p (o c)")
                    for c in range(NC):
                        sl = slice(c * CHUNK, (c + 1) * CHUNK)
                        dve.wait_ge(adj_loaded[c], 16 * (t + 1))
                        nc.vector.tensor_scalar(dropv, adj_sb[:, c, :], 1.0, NEG, ALU.subtract, ALU.mult
                                                ).then_inc(s["chunk_read"], 1)
                        nc.vector.tensor_scalar(scorev, f2row[:, sl], f1t, None, ALU.add).then_inc(s["g_step"], 1)
                        dve.wait_ge(s["g_step"], t * GS + 3 * c + 1)
                        nc.vector.scalar_tensor_tensor(out=scorev, in0=scorev, scalar=SLOPE, in1=scorev,
                                                       op0=ALU.mult, op1=ALU.max).then_inc(s["g_step"], 1)
                        dve.wait_ge(s["g_step"], t * GS + 3 * c + 2)
                        dve.wait_ge(s["chunk_read"], t * NC + c + 1)
                        nc.vector.tensor_tensor(expo[:, sl], scorev, dropv, ALU.add).then_inc(s["g_step"], 1)
                        dve.wait_ge(s["g_step"], t * GS + 3 * c + 3)
                    nc.vector.reduce_max(gm[:, 0:1], expo, AX_X).then_inc(s["g_step"], 1)
                    dve.wait_ge(s["g_step"], t * GS + 3 * NC + 1)
                    nc.vector.tensor_scalar(gm[:, 1:2], gm[:, 0:1], -1.0, None, ALU.mult).then_inc(s["g_shift"], 1)
                    nc.vector.tensor_scalar(gm[:, 3:4], gm[:, 0:1], -NEG / 2, None, ALU.is_gt
                                            ).then_inc(s["g_step"], 1)
                    dve.wait_ge(s["g_step"], t * GS + 3 * NC + 2)
                    dve.wait_ge(s["g_sums"], t + 1)
                    nc.vector.tensor_tensor(gm[:, 4:5], gm[:, 2:3], gm[:, 3:4], ALU.mult).then_inc(s["g_step"], 1)
                    dve.wait_ge(s["g_step"], t * GS + 3 * NC + 3)
                    nc.vector.reciprocal(gm[:, 5:6], gm[:, 4:5]).then_inc(s["g_step"], 1)
                    nc.vector.tensor_scalar(num[:, 0, 0:Fo], acc[:, 0, 0:Fo], gm[:, 3:4], None, ALU.mult
                                            ).then_inc(s["g_step"], 1)
                    dve.wait_ge(s["g_step"], t * GS + 3 * NC + 5)
                    xt = x_sb[:, bass.ds(t, 1), :].rearrange("p o d -> p (o d)")
                    nc.vector.scalar_tensor_tensor(out=xt, in0=num[:, 0, 0:Fo], scalar=gm[:, 5:6], in1=xt,
                                                   op0=ALU.mult, op1=ALU.add).then_inc(s["rows_done"], 1)


_INS = ["x", "adj", "L0_gnn_W", "L0_gnn_a"]


def kernel(**inputs):
    import numpy as _np
    import concourse.bacc as _bacc
    from concourse import mybir as _mybir
    from concourse.bass_utils import run_bass_kernel_spmd as _run

    nc = _bacc.Bacc("TRN2", target_bir_lowering=False, num_devices=1)
    arrays, args = {}, []
    for name in _INS:
        v = _np.ascontiguousarray(inputs[name])
        arrays[f"in_{name}_dram"] = v
        args.append(nc.dram_tensor(f"in_{name}_dram", v.shape, _mybir.dt.from_np(v.dtype), kind="ExternalInput").ap())
    shape = inputs["x"].shape
    args.append(nc.dram_tensor("out_0_dram", shape, _mybir.dt.float32, kind="ExternalOutput").ap())
    gat_kernel(nc, *args)
    r = _run(nc, [arrays], core_ids=[0])
    return r.results[0]["out_0_dram"]
```
